# Optimizing a Trainium2 kernel written in Bass

```python
import numpy as np
import jax
import jax.numpy as jnp

def _softmax(x, axis=-1):
    return jax.nn.softmax(x, axis=axis)

def _gelu(x):
    return jax.nn.gelu(x, approximate=True)

def _silu(x):
    return jax.nn.silu(x)

def _sigmoid(x):
    return jax.nn.sigmoid(x)

def _layernorm(x, axis=-1, eps=1e-05):
    m = jnp.mean(x, axis=axis, keepdims=True)
    v = jnp.var(x, axis=axis, keepdims=True)
    return (x - m) / jnp.sqrt(v + eps)

def _scatter_add(tgt, idx, src, axis=0):
    return tgt.at[idx].add(src)

def _segment_sum(src, seg, n):
    return jax.ops.segment_sum(src, seg, n)
kernel_name = 'mk_adj_preln_d2_adj_r2_489404'

def setup_inputs(seed: int=0):
    np.random.seed(seed)
    _w = jnp.asarray

    def _rec_inputs():
        import jax
        import jax.numpy as jnp
        _gk = jax.random.key(seed)
        x = -0.0002928 + 1 * jax.random.normal(jax.random.fold_in(_gk, 1), (8192, 256), jnp.float32)
        _a = jax.random.bernoulli(jax.random.fold_in(_gk, 2), 0.000244141, (8192, 8192))
        adj = _a.astype(jnp.int32)
        return (x, adj)
    x, adj = _rec_inputs()

    def _L0_gnn_setup():
        import jax, jax.numpy as jnp
        import numpy as np
        N = 4096
        D_IN = 256
        D_OUT = 256
        key = jax.random.key(seed)
        k1, k2, k3, k4 = jax.random.split(key, 4)
        node_feats = jax.random.normal(k1, (N, D_IN), dtype=jnp.float32)
        adj_matrix = jax.random.randint(k2, (N, N), 0, 2, dtype=jnp.int32)
        w_self = jax.random.normal(k3, (D_OUT, D_IN), dtype=jnp.float32) * D_IN ** (-0.5)
        w_neigh = jax.random.normal(k4, (D_OUT, D_IN), dtype=jnp.float32) * D_IN ** (-0.5)
        return {'node_feats': node_feats, 'adj_matrix': adj_matrix, 'w_self': w_self, 'w_neigh': w_neigh}
    _L0_gnn_all = _L0_gnn_setup()
    _L0_gnn_in = {k: v for k, v in _L0_gnn_all.items() if k in ('w_self', 'w_neigh')}
    del _L0_gnn_all

    def _L1_gnn_setup():
        import jax, jax.numpy as jnp
        import numpy as np
        NEG_SLOPE = 0.2
        N, IN_DIM, OUT_DIM, N_HEADS = (2048, 256, 256, 4)
        D_K = OUT_DIM // N_HEADS
        key = jax.random.key(seed)
        k1, k2, k3, k4, k5 = jax.random.split(key, 5)
        H = jax.random.normal(k1, (N, IN_DIM), dtype=jnp.float32)
        A = jax.random.randint(k2, (N, N), 0, 2, dtype=jnp.int32)
        W = jax.random.normal(k3, (IN_DIM, OUT_DIM), dtype=jnp.float32) * (1.0 / np.sqrt(IN_DIM))
        a_l = jax.random.normal(k4, (N_HEADS, D_K), dtype=jnp.float32) * 0.1
        a_r = jax.random.normal(k5, (N_HEADS, D_K), dtype=jnp.float32) * 0.1
        return {'H': H, 'A': A, 'W': W, 'a_l': a_l, 'a_r': a_r}
    _L1_gnn_all = _L1_gnn_setup()
    _L1_gnn_in = {k: v for k, v in _L1_gnn_all.items() if k in ('W', 'a_l', 'a_r')}
    del _L1_gnn_all
    return {'x': x, 'adj': adj, 'L0_gnn_w_self': _L0_gnn_in['w_self'], 'L0_gnn_w_neigh': _L0_gnn_in['w_neigh'], 'L1_gnn_W': _L1_gnn_in['W'], 'L1_gnn_a_l': _L1_gnn_in['a_l'], 'L1_gnn_a_r': _L1_gnn_in['a_r']}

def reference(x, adj, L0_gnn_w_self, L0_gnn_w_neigh, L1_gnn_W, L1_gnn_a_l, L1_gnn_a_r):
    import jax
    import jax.numpy as jnp

    def _L0_gnn_ref(node_feats, adj_matrix, w_self, w_neigh):
        import jax, jax.numpy as jnp
        import numpy as np
        N = 4096
        D_IN = 256
        D_OUT = 256
        adj_f = adj_matrix.astype(node_feats.dtype)
        s = adj_f @ node_feats[:, 0]
        has_neigh = jnp.sum(adj_matrix, axis=1) > 0
        s = jnp.where(has_neigh, s, jnp.zeros_like(s))
        neigh_term = s[:, None] * jnp.sum(w_neigh, axis=1)[None, :]
        return jax.nn.relu(node_feats @ w_self.T + neigh_term)

    def _L1_gnn_ref(H, A, W, a_l, a_r):
        import jax, jax.numpy as jnp
        import numpy as np
        NEG_SLOPE = 0.2
        N, IN_DIM, OUT_DIM, N_HEADS = (2048, 256, 256, 4)
        D_K = OUT_DIM // N_HEADS
        n = H.shape[0]
        mask = A + jnp.eye(n, dtype=A.dtype) > 0
        Wh = (H @ W).reshape(n, N_HEADS, D_K)
        sl = jnp.einsum('nhd,hd->nh', Wh, a_l)
        sr = jnp.einsum('nhd,hd->nh', Wh, a_r)
        e = jax.nn.leaky_relu(sl[:, :, None] + sr.T[None, :, :], negative_slope=NEG_SLOPE)
        e = jnp.where(mask[:, None, :], e, -jnp.inf)
        alpha = jnp.nan_to_num(jax.nn.softmax(e, axis=2), nan=0.0)
        out = jnp.einsum('nhm,mhd->nhd', alpha, Wh).reshape(n, OUT_DIM)
        return jax.nn.elu(out)
    h = jnp.maximum(_layernorm(x, axis=-1), 0.0)
    x = x + _L0_gnn_ref(h, adj, L0_gnn_w_self, L0_gnn_w_neigh)
    h = jnp.maximum(_layernorm(x, axis=-1), 0.0)
    x = x + _L1_gnn_ref(h, adj, L1_gnn_W, L1_gnn_a_l, L1_gnn_a_r)
    return x

_drawn_inputs = setup_inputs


def setup_inputs(seed=0):
    import zlib

    import numpy as np

    out = dict(_drawn_inputs(seed))
    spreads = {}
    factors = {'L1_gnn_a_l': 32.675}
    for name, (base, spread) in spreads.items():
        noise = np.random.default_rng([zlib.crc32(name.encode()), seed]).standard_normal(out[name].shape)
        drawn = base * np.exp(spread * noise) if base else spread * noise
        out[name] = jnp.asarray(drawn.astype(out[name].dtype))
    for name, factor in factors.items():
        out[name] = (out[name] * factor).astype(out[name].dtype)
    return out
```

```python
from contextlib import ExitStack

import concourse.bass as bass
from concourse import mybir

F32 = mybir.dt.float32
I32 = mybir.dt.int32
U32 = mybir.dt.uint32
ALU = mybir.AluOpType
ACT = mybir.ActivationFunctionType
AX = mybir.AxisListType

P = 128
EPS = 1e-5
SLOPE = 0.2
RING = 3
PEELED = 2
SENT = 8
SLOTS = 16
NEAR = 8
SELF = NEAR
CAND = SLOTS + 1
ABSENT = 16384.0
FAR = 1e30


def preln_gnn_gat_kernel(nc, x, adj, w_self, w_neigh, w_gat, a_l, a_r, out):
    N, D = x.shape
    HEADS, DK = a_l.shape
    TILES = N // P
    HALF = N // 2
    DC = D // P
    ROW = D + 2 * HEADS
    SR, SL = D, D + HEADS
    XCH = 8
    ROUNDS = TILES // RING
    assert TILES == RING * ROUNDS + 1 and D == 2 * P and HEADS * DK == D
    FIND, UPD, SCORE, MIX = 8, 4, 6, 4

    h0_dram = nc.dram_tensor("h0_table", [N, 1], F32, kind="Internal").ap()
    row_dram = nc.dram_tensor("row_table", [N, ROW], F32, kind="Internal").ap()
    x_tiles = x.rearrange("(t p) d -> p t d", p=P)

    with ExitStack() as ctx:
        def sb(name, shape, dt=F32):
            return ctx.enter_context(nc.sbuf_tensor(name, shape, dt))

        def ps(name):
            return ctx.enter_context(nc.psum_tensor(name, [P, 512], F32))

        def sem(name):
            return ctx.enter_context(nc.semaphore(name))

        def ring(name, shape, dt=F32):
            return [sb(f"{name}{i}", shape, dt) for i in range(RING)]

        big = sb("big", [P, 2 * RING * (HALF + SENT)], I32)
        A = [big[:, s * (HALF + SENT):(s + 1) * (HALF + SENT)] for s in range(2 * RING)]
        bigf = big[:].bitcast(F32)
        G = [bigf[:, i * CAND * ROW:(i + 1) * CAND * ROW].rearrange("p (j c) -> p j c", c=ROW) for i in range(RING)]
        at = (2 * RING - 1) * (HALF + SENT)
        w_raw, wn_raw, wneighT = (bigf[:, at + i * DC * D:at + (i + 1) * DC * D].rearrange("p (c d) -> p c d", c=DC)
                                  for i in range(3))
        al_b, ar_b, wa_tmp = (bigf[:, at + (3 * DC + i) * D:at + (3 * DC + i + 1) * D] for i in range(3))

        X = sb("x_rows", [P, TILES, D])
        keys_all = sb("keys_all", [P, TILES, SLOTS])
        stat0 = sb("stat0", [P, TILES, 6])
        mean0 = sb("mean0", [P, TILES])
        rstd0 = sb("rstd0", [P, TILES])
        nmr0 = sb("nmr0", [P, TILES])
        tmp0 = sb("tmp0", [P, TILES])
        h0c = sb("h0_columns", [P, TILES])
        h0r = sb("h0_rows", [TILES, P])
        ident = sb("ident", [P, P])
        ones = sb("ones", [P, P])
        eps = sb("eps", [P, 1])
        find8 = sb("find8", [P, 8])
        half_base = sb("half_base", [P, SLOTS])
        absent = sb("absent", [P, SLOTS])
        rown = sb("rown", [P, TILES])
        wselfT = sb("wselfT", [P, DC, D])
        wx = sb("w_gat_and_heads", [P, DC, ROW])
        vsum = sb("w_neigh_sums", [P, D])
        mcol = sb("mcol", [P, P])
        tile_no = sb("tile_no", [1, TILES])
        listed = sb("listed", [1, TILES])
        listed2 = sb("listed2", [1, TILES])
        order = sb("order", [1, TILES])
        dense_tile = sb("dense_tile", [1, TILES], I32)
        dense_sum = sb("dense_sum", [1, 1])
        dense_count = sb("dense_count", [1, 1], I32)
        many = sb("many", [1, TILES, 10], I32)

        found = ring("found", [P, SLOTS], U32)
        pen = ring("pen", [P, SLOTS])
        key = ring("key", [P, SLOTS])
        key2 = ring("key2_", [P, SLOTS])
        skey = ring("skey", [P, SLOTS])
        valid = ring("valid", [P, SLOTS + 2])
        nbr = ring("nbr", [P, SLOTS], U32)
        h0g = ring("h0g", [P, SLOTS])
        svec = ring("s", [P, 1])
        junk = sb("junk", [P, SLOTS])
        h = ring("h", [P, D])
        hT = ring("hT", [P, D])
        y = ring("y", [P, D])
        g = ring("g", [P, D])
        gT = ring("gT", [P, D])
        st1 = ring("st1_", [P, 6])
        mv1 = ring("mv1_", [P, 2])
        sd1 = ring("sd1_", [P, 1])
        rs1 = ring("rs1_", [P, 1])
        nm1 = ring("nm1_", [P, 1])
        rows = ring("rows", [P, ROW])
        bad = ring("bad", [P, CAND])
        gone = ring("gone", [P, SLOTS])
        sc = ring("scores", [P, CAND, HEADS])
        sc2 = ring("leaky", [P, CAND, HEADS])
        mx = ring("mx", [P, HEADS])
        pr = ring("probs", [P, CAND, HEADS])
        den = ring("den", [P, HEADS])
        rden = ring("rden", [P, HEADS])

        p_u = [ps(f"p_u{i}") for i in range(RING)]
        p_hT, p_gT, p_row, p_cnt = ps("p_hT"), ps("p_gT"), ps("p_row"), ps("p_cnt")

        x_in = [sem(f"x_in{i}") for i in range(TILES // XCH)]
        w_in = sem("w_in")
        adj_in = [sem(f"adj_in{i}") for i in range(2 * RING)]
        sentinels = sem("sentinels")
        consts = sem("consts")
        pool_consts = sem("pool_consts")
        stat0_done, ln0_step, sd0_done, h0_done = sem("stat0_done"), sem("ln0_step"), sem("sd0_done"), sem("h0_done")
        h0_turned, h0_copied, h0_out = sem("h0_turned"), sem("h0_copied"), sem("h0_out")
        w_turned, w_copied, wa_step = sem("w_turned"), sem("w_copied"), sem("wa_step")
        vs_done, vs_copied = sem("vs_done"), sem("vs_copied")
        searched, find_step, nbr_ready = sem("searched"), sem("find_step"), sem("nbr_ready")
        counted, count_copied, keys_kept = sem("counted"), sem("count_copied"), sem("keys_kept")
        h0_near = [sem(f"h0_near{i}") for i in range(RING)]
        h0_far_in, h0_far = sem("h0_far_in"), sem("h0_far")
        h_ready, h_turned, hT_ready, u_ready = sem("h_ready"), sem("h_turned"), sem("hT_ready"), sem("u_ready")
        upd_step, mv_ready, sd_ready = sem("upd_step"), sem("mv_ready"), sem("sd_ready")
        rs_ready, norm_ready = sem("rs_ready"), sem("norm_ready")
        g_ready, g_turned, gT_ready = sem("g_ready"), sem("g_turned"), sem("gT_ready")
        row_ready, row_copied = sem("row_ready"), sem("row_copied")
        row_out = [sem(f"row_out{i}") for i in range(RING)]

        def num(k, r):
            return k * RING + r

        def behind(k, r, lag):
            return k + (r - lag) // RING, (r - lag) % RING

        def later_round(k):
            return not isinstance(k, int) or k > 0

        def wait_alone(eng, sem, value):
            if not isinstance(value, int):
                value = eng.to_reg(value)
                eng.wait_ge(consts, 1)
            eng.wait_ge(sem, value)

        def run(eng, *stages):
            def step(k, r):
                for stage, lag in stages:
                    if not isinstance(k, int) or 0 <= num(k, r) - lag < TILES:
                        stage(*behind(k, r, lag))
            for k in range(PEELED):
                for r in range(RING):
                    step(k, r)
            with eng.Fori(PEELED, ROUNDS) as k:
                for r in range(RING):
                    step(k, r)
            for t in range(RING * ROUNDS, TILES + max(lag for _, lag in stages)):
                step(t // RING, t % RING)

        def x_tile(k, r):
            return X[:, bass.ds(num(k, r), 1), :].rearrange("p a d -> p (a d)")

        with nc.Block() as block:

            @block.sync
            def _(sp):
                for c in range(TILES // XCH):
                    sp.dma_start(X[:, c * XCH:(c + 1) * XCH, :], x_tiles[:, c * XCH:(c + 1) * XCH, :]
                                 ).then_inc(x_in[c], 16)

                def load(k, r):
                    for s in range(2):
                        if later_round(k):
                            sp.wait_ge(searched, num(k, r) * 2 + s + 1 - 2 * RING)
                        elif r == RING - 1 and s == 1:
                            sp.wait_ge(vs_copied, 1)
                            sp.wait_ge(w_copied, 2)
                            sp.wait_ge(wa_step, 4 * DC)
                        b = 2 * r + s
                        sp.dma_start(A[b][:, 0:HALF], adj[bass.ds(num(k, r) * P, P), s * HALF:(s + 1) * HALF]
                                     ).then_inc(adj_in[b], 16)
                run(sp, (load, 0))

            @block.gpsimd
            def _(pool):
                nc.gpsimd.memset(ident[:], 0.0).then_inc(pool_consts, 1)
                nc.gpsimd.iota(rown[:], [[-P, TILES]], base=0, channel_multiplier=-1,
                               allow_small_or_imprecise_dtypes=True).then_inc(pool_consts, 1)
                nc.gpsimd.iota(mcol[:], [[1, P]], base=0, channel_multiplier=0,
                               allow_small_or_imprecise_dtypes=True).then_inc(pool_consts, 1)
                pool.wait_ge(pool_consts, 3)
                nc.gpsimd.affine_select(out=ident[:], in_=ident[:], compare_op=ALU.not_equal, fill=1.0,
                                        base=0, pattern=[[-1, P]], channel_multiplier=1).then_inc(pool_consts, 1)
                pool.wait_ge(h0_out, 16)
                pool.wait_ge(consts, 1)

                asked = pool.alloc_register(None)
                pool.reg_mov(asked, 0)

                def ask(r, j, signal):
                    nc.gpsimd.indirect_dma_start(
                        out=h0g[r][:, j:j + 1], out_offset=None, in_=h0_dram[:, :],
                        in_offset=bass.IndirectOffsetOnAxis(ap=nbr[r][:, j:j + 1], axis=0),
                        bounds_check=N - 1, oob_is_err=False).then_inc(signal, 16)

                def gather(k, r):
                    t = num(k, r)
                    pool.wait_ge(nbr_ready, t + 1)
                    if later_round(k):
                        wait_alone(pool, upd_step, (t - RING) * UPD + 1)
                    for j in range(NEAR):
                        ask(r, j, h0_near[r])
                    pool.wait_ge(count_copied, t + 1)
                    full = pool.value_load(many[0:1, bass.ds(t, 1), 0:1], min_val=0, max_val=P)
                    with pool.If(full > 0):
                        for j in range(NEAR, SLOTS):
                            ask(r, j, h0_far_in)
                        pool.reg_add(asked, asked, 16 * (SLOTS - NEAR))
                        pool.wait_ge(h0_far_in, pool.snap(asked))
                        pool.sem_inc(h0_far, 1)
                    with pool.Else():
                        pool.sem_inc(h0_far, 1)
                run(pool, (gather, 0))

            @block.vector
            def _(dve):
                for b in A:
                    nc.vector.memset(b[:, HALF:HALF + SENT], 1).then_inc(sentinels, 1)
                nc.vector.memset(find8[:], 1.0)
                nc.vector.memset(half_base[:, 0:8], 0.0)
                nc.vector.memset(half_base[:, 8:16], -float(HALF))
                nc.vector.memset(absent[:], -ABSENT)
                nc.vector.memset(eps[:], EPS)
                for b in h0g:
                    nc.vector.memset(b[:], 0.0)
                nc.vector.memset(ones[:], 1.0).then_inc(consts, 1)

                dve.wait_ge(w_in, 16 * 5)
                dve.wait_ge(consts, 1)
                n = 0
                for c in range(DC):
                    for at_col, a in ((SR, ar_b), (SL, al_b)):
                        nc.vector.tensor_tensor(wa_tmp, wx[:, c, 0:D], a, ALU.mult).then_inc(wa_step, 1)
                        dve.wait_ge(wa_step, n + 1)
                        nc.vector.tensor_reduce(wx[:, c, at_col:at_col + HEADS],
                                                wa_tmp.rearrange("p (h k) -> p h k", h=HEADS), AX.X, ALU.add
                                                ).then_inc(wa_step, 1)
                        n += 2
                        dve.wait_ge(wa_step, n)

                for c in range(TILES // XCH):
                    dve.wait_ge(x_in[c], 16)
                    for t in range(c * XCH, (c + 1) * XCH):
                        last = nc.vector.bn_stats(stat0[:, t, :], X[:, t, :])
                last.then_inc(stat0_done, 1)
                dve.wait_ge(stat0_done, 1)

                def ln(ins, n):
                    ins.then_inc(ln0_step, 1)
                    dve.wait_ge(ln0_step, n)
                nc.vector.tensor_tensor(mean0[:], stat0[:, :, 1], stat0[:, :, 4], ALU.add)
                nc.vector.tensor_tensor(tmp0[:], stat0[:, :, 1], stat0[:, :, 4], ALU.subtract)
                ln(nc.vector.tensor_tensor(nmr0[:], stat0[:, :, 2], stat0[:, :, 5], ALU.add), 1)
                nc.vector.tensor_scalar(mean0[:], mean0[:], -0.5, None, ALU.mult)
                ln(nc.vector.tensor_tensor(tmp0[:], tmp0[:], tmp0[:], ALU.mult), 2)
                ln(nc.vector.scalar_tensor_tensor(tmp0[:], tmp0[:], D / 4.0, nmr0[:], ALU.mult, ALU.add), 3)
                dve.wait_ge(sd0_done, 1)
                ln(nc.vector.reciprocal(rstd0[:], tmp0[:]), 4)
                nc.vector.tensor_tensor(nmr0[:], mean0[:], rstd0[:], ALU.mult)
                ln(nc.vector.tensor_tensor(h0c[:], X[:, :, 0], rstd0[:], ALU.mult), 5)
                ln(nc.vector.tensor_tensor(h0c[:], h0c[:], nmr0[:], ALU.add), 6)
                nc.vector.tensor_scalar(h0c[:], h0c[:], 0.0, None, ALU.max).then_inc(h0_done, 1)

                def find(k, r):
                    t = num(k, r)
                    f, v = found[r], valid[r]

                    def step(ins, n, wait=True):
                        ins.then_inc(find_step, 1)
                        if wait:
                            wait_alone(dve, find_step, t * FIND + n)
                    for s in range(2):
                        wait_alone(dve, adj_in[2 * r + s], k * 16 + 16)
                        nc.vector.max_index(f[:, 8 * s:8 * s + 8], find8[:], A[2 * r + s]).then_inc(searched, 1)
                    dve.wait_ge(searched, 2 * t + 2)
                    step(nc.vector.scalar_tensor_tensor(pen[r][:], f[:], float(HALF), absent[:], ALU.is_ge, ALU.mult), 1)
                    step(nc.vector.scalar_tensor_tensor(key2[r][:], f[:], -1.0, pen[r][:], ALU.mult, ALU.add), 2)
                    step(nc.vector.tensor_tensor(key[r][:], key2[r][:], half_base[:], ALU.add), 3)
                    if later_round(k):
                        wait_alone(dve, keys_kept, t - RING + 1)
                        wait_alone(dve, counted, t - RING + 1)
                    step(nc.vector.max(skey[r][:, 0:8], key[r][:]), 4)
                    step(nc.vector.match_replace(key2[r][:], skey[r][:, 0:8], key[r][:], -1e9), 5)
                    step(nc.vector.max(skey[r][:, 8:16], key2[r][:]), 6)
                    if later_round(k):
                        dve.wait_ge(h0_near[r], k * 16 * NEAR)
                        dve.wait_ge(h0_far, (t - RING + 1))
                    nc.vector.tensor_scalar(nbr[r][:], skey[r][:], -1.0, None, ALU.mult).then_inc(nbr_ready, 1)
                    step(nc.vector.tensor_scalar(v[:, 0:SLOTS], skey[r][:], 0.5 - N, None, ALU.is_ge), 7, False)
                    step(nc.vector.tensor_scalar(v[:, SLOTS:SLOTS + 2], f[:, 7:16:8], HALF - 0.5, None, ALU.is_lt), 8, False)

                def update(k, r):
                    t = num(k, r)

                    def step(ins, n):
                        ins.then_inc(upd_step, 1)
                        wait_alone(dve, upd_step, t * UPD + n)
                    dve.wait_ge(h0_near[r], (k + 1) * 16 * NEAR)
                    dve.wait_ge(h0_far, (t + 1))
                    dve.wait_ge(find_step, (t + 1) * FIND)
                    step(nc.vector.tensor_tensor_reduce(junk[:], h0g[r][:], valid[r][:, 0:SLOTS], 1.0, 0.0,
                                                        ALU.mult, ALU.add, svec[r][:]), 1)
                    if isinstance(k, int) and t == 0:
                        dve.wait_ge(vs_copied, 1)
                    dve.wait_ge(u_ready, t + 1)
                    step(nc.vector.scalar_tensor_tensor(y[r][:], vsum[:], svec[r][:], p_u[r][:, 0:D], ALU.mult, ALU.add), 2)
                    step(nc.vector.scalar_tensor_tensor(x_tile(k, r), y[r][:], 0.0, x_tile(k, r), ALU.max, ALU.add), 3)
                    step(nc.vector.bn_stats(st1[r][:], x_tile(k, r)), 4)
                    nc.vector.bn_aggr(mv1[r][:], st1[r][:]).then_inc(mv_ready, 1)

                def norm(k, r):
                    t = num(k, r)
                    dve.wait_ge(sd_ready, t + 1)
                    nc.vector.reciprocal(rs1[r][:], sd1[r][:]).then_inc(rs_ready, 1)
                    dve.wait_ge(rs_ready, t + 1)
                    nc.vector.scalar_tensor_tensor(nm1[r][:], mv1[r][:, 0:1], -1.0, rs1[r][:], ALU.mult, ALU.mult
                                                   ).then_inc(norm_ready, 1)
                run(dve, (find, 0), (norm, 3), (update, 2))

            @block.scalar
            def _(act):
                act.dma_start(w_raw, w_self.rearrange("(c p) d -> p c d", p=P)).then_inc(w_in, 16)
                act.dma_start(wn_raw, w_neigh.rearrange("(c p) d -> p c d", p=P)).then_inc(w_in, 16)
                act.dma_start(wx[:, :, 0:D], w_gat.rearrange("(c p) d -> p c d", p=P)).then_inc(w_in, 16)
                act.dma_start(al_b, a_l.rearrange("(o h) k -> o (h k)", o=1).broadcast_to([P, D])).then_inc(w_in, 16)
                act.dma_start(ar_b, a_r.rearrange("(o h) k -> o (h k)", o=1).broadcast_to([P, D])).then_inc(w_in, 16)
                for i, dst in enumerate((wselfT[:], wneighT)):
                    act.wait_ge(w_turned, i + 1)
                    nc.scalar.copy(dst.rearrange("p c d -> p (c d)"), p_u[i][:]).then_inc(w_copied, 1)
                act.wait_ge(vs_done, 1)
                nc.scalar.copy(vsum[:], p_u[2][:, 0:D]).then_inc(vs_copied, 1)
                act.wait_ge(ln0_step, 3)
                nc.scalar.activation(tmp0[:], tmp0[:], ACT.Sqrt, bias=eps[:], scale=1.0 / D).then_inc(sd0_done, 1)
                act.wait_ge(h0_turned, 1)
                nc.scalar.copy(h0r[:], p_cnt[0:TILES, 0:P]).then_inc(h0_copied, 1)
                act.wait_ge(h0_copied, 1)
                act.dma_start(h0_dram.rearrange("(t p) o -> t (p o)", p=P), h0r[:]).then_inc(h0_out, 16)

                def first_norm(k, r):
                    t = num(k, r)
                    if later_round(k):
                        act.wait_ge(h_turned, t - RING + 1)
                    nc.scalar.activation(h[r][:], x_tile(k, r), ACT.Relu, bias=nmr0[:, bass.ds(t, 1)],
                                         scale=rstd0[:, bass.ds(t, 1)]).then_inc(h_ready, 1)
                    act.wait_ge(h_turned, t + 1)
                    if later_round(k):
                        act.wait_ge(u_ready, t - RING + 1)
                    nc.scalar.copy(hT[r][:], p_hT[:, 0:D]).then_inc(hT_ready, 1)

                def keep(k, r):
                    t = num(k, r)
                    act.wait_ge(find_step, t * FIND + 6)
                    nc.scalar.copy(keys_all[:, bass.ds(t, 1), :].rearrange("p a j -> p (a j)"), skey[r][:]
                                   ).then_inc(keys_kept, 1)
                    act.wait_ge(counted, t + 1)
                    nc.scalar.copy(many[0:1, bass.ds(t, 1), :].rearrange("p a j -> p (a j)"), p_cnt[0:1, 0:10]
                                   ).then_inc(count_copied, 1)

                def deviation(k, r):
                    act.wait_ge(mv_ready, num(k, r) + 1)
                    nc.scalar.activation(sd1[r][:], mv1[r][:, 1:2], ACT.Sqrt, bias=eps[:]).then_inc(sd_ready, 1)

                def second_norm(k, r):
                    t = num(k, r)
                    act.wait_ge(norm_ready, t + 1)
                    if later_round(k):
                        act.wait_ge(g_turned, t - RING + 1)
                    nc.scalar.activation(g[r][:], x_tile(k, r), ACT.Relu, bias=nm1[r][:], scale=rs1[r][:]
                                         ).then_inc(g_ready, 1)
                    act.wait_ge(g_turned, t + 1)
                    if later_round(k):
                        act.wait_ge(row_ready, t - RING + 1)
                    nc.scalar.copy(gT[r][:], p_gT[:, 0:D]).then_inc(gT_ready, 1)

                def write_rows(k, r):
                    t = num(k, r)
                    act.wait_ge(row_ready, t + 1)
                    if later_round(k):
                        act.wait_ge(row_out[r], k * 16)
                    nc.scalar.copy(rows[r][:], p_row[:, 0:ROW]).then_inc(row_copied, 1)
                    act.wait_ge(row_copied, t + 1)
                    act.dma_start(row_dram[bass.ds(t * P, P), :], rows[r][:]).then_inc(row_out[r], 16)
                run(act, (first_norm, 0), (keep, 0), (second_norm, 3), (write_rows, 3), (deviation, 2))
                for r in range(RING):
                    act.wait_ge(row_out[r], 16 * len(range(r, TILES, RING)))

            @block.tensor
            def _(pe):
                pe.wait_ge(w_in, 16 * 5)
                pe.wait_ge(pool_consts, 4)
                for i, raw in enumerate((w_raw, wn_raw)):
                    for c in range(DC):
                        for o in range(DC):
                            at_col = c * D + o * P
                            last = nc.tensor.transpose(p_u[i][:, at_col:at_col + P], raw[:, o, c * P:(c + 1) * P], ident[:])
                    last.then_inc(w_turned, 1)
                pe.wait_ge(w_copied, 2)
                pe.wait_ge(consts, 1)
                for c in range(DC):
                    last = nc.tensor.matmul(p_u[2][:, 0:D], ones[:], wneighT[:, c, :], start=(c == 0), stop=(c == DC - 1))
                last.then_inc(vs_done, 1)
                pe.wait_ge(h0_done, 1)
                nc.tensor.transpose(p_cnt[0:TILES, 0:P], h0c[:], ident[:]).then_inc(h0_turned, 1)
                pe.wait_ge(h0_copied, 1)
                pe.wait_ge(vs_copied, 1)
                pe.wait_ge(wa_step, 4 * DC)

                def self_term(k, r):
                    t = num(k, r)
                    pe.wait_ge(h_ready, t + 1)
                    if not (isinstance(t, int) and t == 0):
                        pe.wait_ge(hT_ready, t)
                    for c in range(DC):
                        last = nc.tensor.transpose(p_hT[:, c * P:(c + 1) * P], h[r][:, c * P:(c + 1) * P], ident[:])
                    last.then_inc(h_turned, 1)
                    pe.wait_ge(hT_ready, t + 1)
                    if later_round(k):
                        pe.wait_ge(upd_step, (t - RING) * UPD + 2)
                    for c in range(DC):
                        last = nc.tensor.matmul(p_u[r][:, 0:D], hT[r][:, c * P:(c + 1) * P], wselfT[:, c, :],
                                                start=(c == 0), stop=(c == DC - 1))
                    last.then_inc(u_ready, 1)

                def count(k, r):
                    t = num(k, r)
                    pe.wait_ge(find_step, (t + 1) * FIND)
                    if not (isinstance(t, int) and t == 0):
                        pe.wait_ge(count_copied, t)
                    nc.tensor.matmul(p_cnt[:, 0:10], ones[:], valid[r][:, NEAR:SLOTS + 2], start=True, stop=True
                                     ).then_inc(counted, 1)

                def table_rows(k, r):
                    t = num(k, r)
                    pe.wait_ge(g_ready, t + 1)
                    if not (isinstance(t, int) and t == 0):
                        pe.wait_ge(gT_ready, t)
                    for c in range(DC):
                        last = nc.tensor.transpose(p_gT[:, c * P:(c + 1) * P], g[r][:, c * P:(c + 1) * P], ident[:])
                    last.then_inc(g_turned, 1)
                    pe.wait_ge(gT_ready, t + 1)
                    if not (isinstance(t, int) and t == 0):
                        pe.wait_ge(row_copied, t)
                    for c in range(DC):
                        last = nc.tensor.matmul(p_row[:, 0:ROW], gT[r][:, c * P:(c + 1) * P], wx[:, c, :],
                                                start=(c == 0), stop=(c == DC - 1))
                    last.then_inc(row_ready, 1)
                run(pe, (self_term, 0), (count, 0), (table_rows, 3))

        tiles_listed, list_step = sem("tiles_listed"), sem("list_step")
        d_free, d_in, d_h, d_hT, d_hT_copied, d_u = (sem(f"d_{n}") for n in ("free", "in", "h", "hT", "hT_copied", "u"))
        d_step, d_stats, d_sd, d_norm = (sem(f"d_{n}") for n in ("step", "stats", "sd", "norm"))
        d_g, d_gT, d_gT_copied, d_row, d_row_copied, d_out = (
            sem(f"d_{n}") for n in ("g", "gT", "gT_copied", "row", "row_copied", "out"))
        D_STEPS = 7
        h0_all = [bigf[:, (2 + s) * (HALF + SENT):(2 + s) * (HALF + SENT) + HALF] for s in range(2)]
        part = sb("part", [P, 2])

        def each_dense_tile(eng, body):
            eng.wait_ge(tiles_listed, 1)
            count = eng.value_load(dense_count[0:1, 0:1], min_val=0, max_val=TILES)
            with eng.If(count > 0):
                with eng.Fori(0, count) as i:
                    body(i, eng.value_load(dense_tile[0:1, bass.ds(i, 1)], min_val=0, max_val=TILES - 1))
                eng.wait_ge(tiles_listed, 1)

        def x_at(t):
            return X[:, bass.ds(t, 1), :].rearrange("p a d -> p (a d)")

        with nc.Block() as block:

            @block.sync
            def _(sp):
                def load(i, t):
                    sp.wait_ge(d_free, i + 1)
                    sp.dma_start(x_at(t), x[bass.ds(t * P, P), :]).then_inc(d_in, 16)
                    for s in range(2):
                        sp.dma_start(A[s][:, 0:HALF], adj[bass.ds(t * P, P), s * HALF:(s + 1) * HALF]).then_inc(d_in, 16)
                        sp.dma_start(h0_all[s], h0_dram[s * HALF:(s + 1) * HALF, :].rearrange("n o -> o n")
                                     .broadcast_to([P, HALF])).then_inc(d_in, 16)
                each_dense_tile(sp, load)

            @block.vector
            def _(dve):
                def step(ins, n):
                    ins.then_inc(list_step, 1)
                    dve.wait_ge(list_step, n)
                step(nc.vector.tensor_tensor(listed[:], many[:, :, SLOTS - NEAR], many[:, :, SLOTS - NEAR + 1], ALU.add), 1)
                step(nc.vector.tensor_scalar(tile_no[:], rown[0:1, :], -1.0 / P, 1.0, ALU.mult, ALU.add), 2)
                step(nc.vector.tensor_scalar(listed2[:], listed[:], 0.5, None, ALU.is_gt), 3)
                step(nc.vector.tensor_reduce(dense_sum[:], listed2[:], AX.X, ALU.add), 4)
                step(nc.vector.tensor_tensor(listed[:], listed2[:], tile_no[:], ALU.mult), 5)
                n, src, dst = 5, listed, listed2
                for c in range(TILES // 8):
                    step(nc.vector.max(order[:, 8 * c:8 * c + 8], src[:]), n + 1)
                    step(nc.vector.match_replace(dst[:], order[:, 8 * c:8 * c + 8], src[:], -1.0), n + 2)
                    n, src, dst = n + 2, dst, src
                nc.vector.tensor_copy(dense_count[:], dense_sum[:])
                nc.vector.tensor_scalar(dense_tile[:], order[:], -1.0, 0.0, ALU.add, ALU.max).then_inc(tiles_listed, 1)
                dve.sem_inc(d_free, 1)

                def sums(i, t):
                    def step(ins, n):
                        ins.then_inc(d_step, 1)
                        wait_alone(dve, d_step, i * D_STEPS + n)
                    dve.wait_ge(d_in, (i + 1) * 16 * 5)
                    for s in range(2):
                        step(nc.vector.tensor_tensor_reduce(h0_all[s], A[s][:, 0:HALF], h0_all[s], 1.0, 0.0,
                                                            ALU.mult, ALU.add, part[:, s:s + 1]), s + 1)
                    step(nc.vector.tensor_tensor(svec[0][:], part[:, 0:1], part[:, 1:2], ALU.add), 3)
                    dve.wait_ge(d_u, i + 1)
                    step(nc.vector.scalar_tensor_tensor(y[0][:], vsum[:], svec[0][:], p_u[0][:, 0:D], ALU.mult, ALU.add), 4)
                    step(nc.vector.scalar_tensor_tensor(x_at(t), y[0][:], 0.0, x_at(t), ALU.max, ALU.add), 5)
                    step(nc.vector.bn_stats(st1[0][:], x_at(t)), 6)
                    nc.vector.bn_aggr(mv1[0][:], st1[0][:]).then_inc(d_stats, 1)
                    dve.wait_ge(d_sd, i + 1)
                    step(nc.vector.reciprocal(rs1[0][:], sd1[0][:]), 7)
                    nc.vector.scalar_tensor_tensor(nm1[0][:], mv1[0][:, 0:1], -1.0, rs1[0][:], ALU.mult, ALU.mult
                                                   ).then_inc(d_norm, 1)
                each_dense_tile(dve, sums)

            @block.scalar
            def _(act):
                def norms(i, t):
                    wait_alone(act, d_in, (i + 1) * 16 * 5)
                    nc.scalar.activation(h[0][:], x_at(t), ACT.Relu, bias=nmr0[:, bass.ds(t, 1)],
                                         scale=rstd0[:, bass.ds(t, 1)]).then_inc(d_h, 1)
                    act.wait_ge(d_hT, i + 1)
                    nc.scalar.copy(hT[0][:], p_hT[:, 0:D]).then_inc(d_hT_copied, 1)
                    act.wait_ge(d_stats, i + 1)
                    nc.scalar.activation(sd1[0][:], mv1[0][:, 1:2], ACT.Sqrt, bias=eps[:]).then_inc(d_sd, 1)
                    wait_alone(act, d_norm, i + 1)
                    nc.scalar.activation(g[0][:], x_at(t), ACT.Relu, bias=nm1[0][:], scale=rs1[0][:]).then_inc(d_g, 1)
                    act.wait_ge(d_gT, i + 1)
                    nc.scalar.copy(gT[0][:], p_gT[:, 0:D]).then_inc(d_gT_copied, 1)
                    act.wait_ge(d_row, i + 1)
                    nc.scalar.copy(rows[0][:], p_row[:, 0:ROW]).then_inc(d_row_copied, 1)
                    act.wait_ge(d_row_copied, i + 1)
                    act.dma_start(row_dram[bass.ds(t * P, P), :], rows[0][:]).then_inc(d_out, 16)
                    act.wait_ge(d_out, (i + 1) * 16)
                    act.sem_inc(d_free, 1)
                each_dense_tile(act, norms)

            @block.tensor
            def _(pe):
                def products(i, t):
                    pe.wait_ge(d_h, i + 1)
                    for c in range(DC):
                        last = nc.tensor.transpose(p_hT[:, c * P:(c + 1) * P], h[0][:, c * P:(c + 1) * P], ident[:])
                    last.then_inc(d_hT, 1)
                    pe.wait_ge(d_hT_copied, i + 1)
                    for c in range(DC):
                        last = nc.tensor.matmul(p_u[0][:, 0:D], hT[0][:, c * P:(c + 1) * P], wselfT[:, c, :],
                                                start=(c == 0), stop=(c == DC - 1))
                    last.then_inc(d_u, 1)
                    pe.wait_ge(d_g, i + 1)
                    for c in range(DC):
                        last = nc.tensor.transpose(p_gT[:, c * P:(c + 1) * P], g[0][:, c * P:(c + 1) * P], ident[:])
                    last.then_inc(d_gT, 1)
                    pe.wait_ge(d_gT_copied, i + 1)
                    for c in range(DC):
                        last = nc.tensor.matmul(p_row[:, 0:ROW], gT[0][:, c * P:(c + 1) * P], wx[:, c, :],
                                                start=(c == 0), stop=(c == DC - 1))
                    last.then_inc(d_row, 1)
                each_dense_tile(pe, products)

        cleared, lists_ready, self_in = sem("cleared"), sem("lists_ready"), [sem(f"self_in{i}") for i in range(RING)]
        near_in, far_in = [sem(f"near_in{i}") for i in range(RING)], sem("far_in")
        far_rows_in = sem("far_rows_in")
        score_step, shifted, exp_done = sem("score_step"), sem("shifted"), sem("exp_done")
        mix_step, mixed, low_ready, low_exp = sem("mix_step"), sem("mixed"), sem("low_ready"), sem("low_exp")
        res_step, res_ready = sem("res_step"), sem("res_ready")
        res_out = [sem(f"res_out{i}") for i in range(RING)]
        lists, mixv, low, res = nbr, h, y, g

        with nc.Block() as block:

            @block.sync
            def _(sp):
                sp.wait_ge(cleared, 1)

                def own_rows(k, r):
                    t = num(k, r)
                    if later_round(k):
                        sp.wait_ge(mixed, t - RING + 1)
                    sp.dma_start(G[r][:, SELF, :], row_dram[bass.ds(t * P, P), :]).then_inc(self_in[r], 16)

                def write(k, r):
                    t = num(k, r)
                    sp.wait_ge(res_ready, t + 1)
                    sp.dma_start(out[bass.ds(t * P, P), :], res[r][:]).then_inc(res_out[r], 16)
                run(sp, (own_rows, 0), (write, 3))
                for r in range(RING):
                    sp.wait_ge(res_out[r], 16 * len(range(r, TILES, RING)))

            @block.gpsimd
            def _(pool):
                pool.wait_ge(cleared, 1)

                asked = pool.alloc_register(None)
                pool.reg_mov(asked, 0)

                def ask(r, j, signal):
                    place = j if j < NEAR else j + 1
                    nc.gpsimd.indirect_dma_start(
                        out=G[r][:, place, :], out_offset=None, in_=row_dram[:, :],
                        in_offset=bass.IndirectOffsetOnAxis(ap=lists[r][:, j:j + 1], axis=0),
                        bounds_check=N - 1, oob_is_err=False).then_inc(signal, 16)

                def gather(k, r):
                    t = num(k, r)
                    full = pool.value_load(many[0:1, bass.ds(t, 1), 0:1], min_val=0, max_val=P)
                    wait_alone(pool, lists_ready, t + 1)
                    if later_round(k):
                        wait_alone(pool, mixed, t - RING + 1)
                    for j in range(NEAR):
                        ask(r, j, near_in[r])
                    with pool.If(full > 0):
                        for j in range(NEAR, SLOTS):
                            ask(r, j, far_rows_in)
                        pool.reg_add(asked, asked, 16 * (SLOTS - NEAR))
                        pool.wait_ge(far_rows_in, pool.snap(asked))
                        pool.sem_inc(far_in, 1)
                    with pool.Else():
                        pool.sem_inc(far_in, 1)
                run(pool, (gather, 0))

            @block.scalar
            def _(act):
                def list_rows(k, r):
                    t = num(k, r)
                    if later_round(k):
                        act.wait_ge(near_in[r], k * 16 * NEAR)
                        act.wait_ge(far_in, (t - RING + 1))
                    nc.scalar.activation(lists[r][:], keys_all[:, bass.ds(t, 1), :].rearrange("p a j -> p (a j)"),
                                         ACT.Copy, scale=-1.0).then_inc(lists_ready, 1)

                def exps(k, r):
                    act.wait_ge(shifted, num(k, r) + 1)
                    nc.scalar.activation(pr[r][:], sc[r][:], ACT.Exp).then_inc(exp_done, 1)

                def elu_exp(k, r):
                    t = num(k, r)
                    act.wait_ge(low_ready, t + 1)
                    nc.scalar.activation(low[r][:], low[r][:], ACT.Exp).then_inc(low_exp, 1)
                run(act, (list_rows, 0), (exps, 1), (elu_exp, 2))

            @block.vector
            def _(dve):
                for i in range(RING):
                    nc.vector.memset(bad[i][:], 0.0)
                last = nc.vector.memset(bigf[:, 0:RING * CAND * ROW], 0.0)
                last.then_inc(cleared, 1)
                dve.wait_ge(cleared, 1)

                def heads(ap, n):
                    return ap.rearrange("p (o h) -> p o h", o=1).broadcast_to([P, n, HEADS])

                def score(k, r):
                    t = num(k, r)

                    def step(ins, n):
                        ins.then_inc(score_step, 1)
                        dve.wait_ge(score_step, t * SCORE + n)
                    keys = keys_all[:, bass.ds(t, 1), :].rearrange("p a j -> p (a j)")
                    step(nc.vector.tensor_scalar(gone[r][:], keys, 0.5 - N, None, ALU.is_lt), 1)
                    nc.vector.scalar_tensor_tensor(bad[r][:, 0:NEAR], keys[:, 0:NEAR], rown[:, bass.ds(t, 1)],
                                                   gone[r][:, 0:NEAR], ALU.is_equal, ALU.add)
                    nc.vector.scalar_tensor_tensor(bad[r][:, NEAR + 1:CAND], keys[:, NEAR:SLOTS], rown[:, bass.ds(t, 1)],
                                                   gone[r][:, NEAR:SLOTS], ALU.is_equal, ALU.add)
                    dve.wait_ge(self_in[r], (k + 1) * 16)
                    dve.wait_ge(near_in[r], (k + 1) * 16 * NEAR)
                    dve.wait_ge(far_in, (t + 1))
                    step(nc.vector.tensor_tensor(sc[r][:], G[r][:, :, SR:SR + HEADS], heads(G[r][:, SELF, SL:SL + HEADS], CAND),
                                                 ALU.add), 2)
                    step(nc.vector.scalar_tensor_tensor(sc2[r][:], sc[r][:], SLOPE, sc[r][:], ALU.mult, ALU.max), 3)
                    out_of_it = bad[r][:].rearrange("p (j o) -> p j o", o=1).broadcast_to([P, CAND, HEADS])
                    step(nc.vector.scalar_tensor_tensor(sc2[r][:], out_of_it, -FAR, sc2[r][:], ALU.mult, ALU.add), 4)
                    step(nc.vector.tensor_reduce(mx[r][:], sc2[r][:].rearrange("p j h -> p h j"), AX.X, ALU.max), 5)
                    nc.vector.tensor_tensor(sc[r][:], sc2[r][:], heads(mx[r][:], CAND), ALU.subtract).then_inc(shifted, 1)
                    dve.sem_inc(score_step, 1)

                def mix(k, r):
                    t = num(k, r)

                    def step(ins, n):
                        ins.then_inc(mix_step, 1)
                        dve.wait_ge(mix_step, t * MIX + n)
                    dve.wait_ge(exp_done, t + 1)
                    step(nc.vector.tensor_reduce(den[r][:], pr[r][:].rearrange("p j h -> p h j"), AX.X, ALU.add), 1)
                    step(nc.vector.reciprocal(rden[r][:], den[r][:]), 2)
                    step(nc.vector.tensor_tensor(pr[r][:], pr[r][:], heads(rden[r][:], CAND), ALU.mult), 3)

                    def weigh(n):
                        w = pr[r][:, 0:n, :].rearrange("p j (h o) -> p j h o", o=1).broadcast_to([P, n, HEADS, DK])
                        wh = G[r][:, 0:n, 0:D]
                        step(nc.vector.tensor_tensor(wh.rearrange("p j (h k) -> p j h k", h=HEADS),
                                                     wh.rearrange("p j (h k) -> p j h k", h=HEADS), w, ALU.mult), 4)
                        nc.vector.tensor_reduce(mixv[r][:], wh.rearrange("p j d -> p d j"), AX.X, ALU.add
                                                ).then_inc(mixed, 1)
                    full = dve.value_load(many[0:1, bass.ds(t, 1), 0:1], min_val=0, max_val=P)
                    with dve.If(full > 0):
                        weigh(CAND)
                    with dve.Else():
                        weigh(SELF + 1)
                    dve.wait_ge(mixed, t + 1)
                    nc.vector.tensor_scalar(low[r][:], mixv[r][:], 0.0, None, ALU.min).then_inc(low_ready, 1)

                def finish(k, r):
                    t = num(k, r)
                    if later_round(k):
                        dve.wait_ge(res_out[r], k * 16)
                    nc.vector.scalar_tensor_tensor(res[r][:], mixv[r][:], 0.0, x_tile(k, r), ALU.max, ALU.add
                                                   ).then_inc(res_step, 1)
                    dve.wait_ge(res_step, t + 1)
                    dve.wait_ge(low_exp, t + 1)
                    nc.vector.scalar_tensor_tensor(res[r][:], low[r][:], -1.0, res[r][:], ALU.add, ALU.add
                                                   ).then_inc(res_ready, 1)
                run(dve, (score, 0), (mix, 1), (finish, 2))

        e_free, e_in, e_block_in, e_block_free = sem("e_free"), sem("e_in"), sem("e_block_in"), sem("e_block_free")
        e_diag, e_spread, e_args, e_exps, e_turned, e_copied, e_product = (
            sem(f"e_{n}") for n in ("diag", "spread", "args", "exps", "turned", "copied", "product"))
        e_step, e_tile_step, e_low, e_low_exp, e_res, e_out = (
            sem(f"e_{n}") for n in ("step", "tile_step", "low", "low_exp", "res", "out"))
        BLOCKS = HALF // P
        E_STEPS, E_TILE_STEPS = 12, 7
        off = [2 * (HALF + SENT)]

        def take(width):
            off[0] += width
            return bigf[:, off[0] - width:off[0]]
        e_self, e_rows, e_mask, e_neg = take(ROW), take(ROW), take(P), take(P)
        e_dg, e_raw, e_sc, e_p, e_pT = (take(HEADS * P) for _ in range(5))
        e_rel, e_mx, e_bm, e_new, e_dc, e_corr, e_sum, e_l = (take(HEADS) for _ in range(8))
        e_acc, e_lowv = take(D), take(D)

        def per_head(ap):
            return ap.rearrange("p (h m) -> p h m", h=HEADS)

        def over(ap, n):
            return ap.rearrange("p (h o) -> p h o", o=1).broadcast_to([P, HEADS, n])

        def every_head(ap):
            return ap.rearrange("p (o m) -> p o m", o=1).broadcast_to([P, HEADS, P])

        def each_block(eng, i, body):
            for s in range(2):
                with eng.Fori(0, BLOCKS) as b:
                    body((i * 2 + s) * BLOCKS + b, s, b)

        with nc.Block() as block:

            @block.sync
            def _(sp):
                def load(i, t):
                    sp.wait_ge(e_free, i + 1)
                    for s in range(2):
                        sp.dma_start(A[s][:, 0:HALF], adj[bass.ds(t * P, P), s * HALF:(s + 1) * HALF]).then_inc(e_in, 16)
                    sp.dma_start(e_self, row_dram[bass.ds(t * P, P), :]).then_inc(e_in, 16)

                    def block_rows(n, s, b):
                        sp.wait_ge(e_block_free, n + 1)
                        sp.dma_start(e_rows, row_dram[bass.ds(b * P + s * HALF, P), :]).then_inc(e_block_in, 16)
                    each_block(sp, i, block_rows)
                    sp.wait_ge(e_res, i + 1)
                    sp.dma_start(out[bass.ds(t * P, P), :], res[0][:]).then_inc(e_out, 16)
                    sp.wait_ge(e_out, (i + 1) * 16)
                    sp.sem_inc(e_free, 1)
                each_dense_tile(sp, load)

            @block.vector
            def _(dve):
                dve.sem_inc(e_free, 1)
                dve.sem_inc(e_block_free, 1)

                def attend(i, t):
                    def tile_step(ins, n):
                        ins.then_inc(e_tile_step, 1)
                        wait_alone(dve, e_tile_step, i * E_TILE_STEPS + n)
                    dve.wait_ge(e_in, (i + 1) * 16 * 3)
                    nc.vector.memset(e_l, 1.0)
                    nc.vector.tensor_copy(e_acc, e_self[:, 0:D])
                    nc.vector.tensor_scalar(e_rel[:, 0:1], rown[:, bass.ds(t, 1)], -1.0, None, ALU.mult)
                    tile_step(nc.vector.tensor_tensor(e_bm, e_self[:, SR:SR + HEADS], e_self[:, SL:SL + HEADS], ALU.add), 1)
                    tile_step(nc.vector.scalar_tensor_tensor(e_mx, e_bm, SLOPE, e_bm, ALU.mult, ALU.max), 2)

                    def one_block(n, s, b):
                        def step(ins, m):
                            ins.then_inc(e_step, 1)
                            wait_alone(dve, e_step, n * E_STEPS + m)
                        wait_alone(dve, e_block_in, (n + 1) * 16)
                        nc.vector.tensor_tensor(per_head(e_dg), every_head(ident[:]), over(e_rows[:, SR:SR + HEADS], P),
                                                ALU.mult).then_inc(e_diag, 1)
                        step(nc.vector.scalar_tensor_tensor(e_mask, mcol[:], e_rel[:, 0:1], A[s][:, bass.ds(b * P, P)],
                                                            ALU.not_equal, ALU.mult), 1)
                        nc.vector.tensor_scalar(e_rel[:, 0:1], e_rel[:, 0:1], -float(P), None, ALU.add)
                        step(nc.vector.tensor_scalar(e_neg, e_mask, -1.0, FAR, ALU.add, ALU.mult), 2)
                        wait_alone(dve, e_spread, n + 1)
                        step(nc.vector.tensor_tensor(per_head(e_raw), per_head(p_u[0][:]), over(e_self[:, SL:SL + HEADS], P),
                                                     ALU.add), 3)
                        step(nc.vector.scalar_tensor_tensor(e_sc, e_raw, SLOPE, e_raw, ALU.mult, ALU.max), 4)
                        step(nc.vector.tensor_tensor(per_head(e_raw), per_head(e_sc), every_head(e_neg), ALU.add), 5)
                        step(nc.vector.tensor_reduce(e_bm, per_head(e_raw), AX.X, ALU.max), 6)
                        step(nc.vector.tensor_tensor(e_new, e_mx, e_bm, ALU.max), 7)
                        nc.vector.tensor_tensor(e_dc, e_mx, e_new, ALU.subtract)
                        step(nc.vector.tensor_tensor(per_head(e_sc), per_head(e_raw), over(e_new, P), ALU.subtract), 8)
                        nc.vector.tensor_copy(e_mx, e_new).then_inc(e_args, 1)
                        wait_alone(dve, e_exps, n + 1)
                        nc.vector.tensor_tensor(per_head(e_acc), per_head(e_acc), over(e_corr, DK), ALU.mult)
                        step(nc.vector.tensor_tensor(e_l, e_l, e_corr, ALU.mult), 9)
                        step(nc.vector.tensor_reduce(e_sum, per_head(e_p), AX.X, ALU.add), 10)
                        step(nc.vector.tensor_tensor(e_l, e_l, e_sum, ALU.add), 11)
                        wait_alone(dve, e_product, n + 1)
                        nc.vector.tensor_tensor(e_acc, e_acc, p_u[2][:, 0:D], ALU.add).then_inc(e_block_free, 1)
                        wait_alone(dve, e_block_free, n + 2)
                        dve.sem_inc(e_step, 1)
                    each_block(dve, i, one_block)
                    tile_step(nc.vector.reciprocal(e_sum, e_l), 3)
                    tile_step(nc.vector.tensor_tensor(per_head(e_acc), per_head(e_acc), over(e_sum, DK), ALU.mult), 4)
                    nc.vector.tensor_scalar(e_lowv, e_acc, 0.0, None, ALU.min).then_inc(e_low, 1)
                    tile_step(nc.vector.scalar_tensor_tensor(res[0][:], e_acc, 0.0, x_at(t), ALU.max, ALU.add), 5)
                    wait_alone(dve, e_low_exp, i + 1)
                    tile_step(nc.vector.scalar_tensor_tensor(res[0][:], e_lowv, -1.0, res[0][:], ALU.add, ALU.add), 6)
                    dve.sem_inc(e_tile_step, 1)
                    dve.sem_inc(e_res, 1)
                each_dense_tile(dve, attend)

            @block.scalar
            def _(act):
                def exps(i, t):
                    def one_block(n, s, b):
                        act.wait_ge(e_args, n + 1)
                        nc.scalar.activation(e_corr, e_dc, ACT.Exp)
                        nc.scalar.activation(e_p, e_sc, ACT.Exp).then_inc(e_exps, 1)
                        act.wait_ge(e_turned, n + 1)
                        nc.scalar.copy(e_pT, p_u[1][:]).then_inc(e_copied, 1)
                    each_block(act, i, one_block)
                    act.wait_ge(e_low, i + 1)
                    nc.scalar.activation(e_lowv, e_lowv, ACT.Exp).then_inc(e_low_exp, 1)
                each_dense_tile(act, exps)

            @block.tensor
            def _(pe):
                def products(i, t):
                    def one_block(n, s, b):
                        pe.wait_ge(e_diag, n + 1)
                        nc.tensor.matmul(p_u[0][:], ones[:], e_dg, start=True, stop=True).then_inc(e_spread, 1)
                        pe.wait_ge(e_exps, n + 1)
                        for q in range(HEADS):
                            last = nc.tensor.transpose(p_u[1][:, q * P:(q + 1) * P], e_p[:, q * P:(q + 1) * P], ident[:])
                        last.then_inc(e_turned, 1)
                        pe.wait_ge(e_copied, n + 1)
                        for q in range(HEADS):
                            last = nc.tensor.matmul(p_u[2][:, q * DK:(q + 1) * DK], e_pT[:, q * P:(q + 1) * P],
                                                    e_rows[:, q * DK:(q + 1) * DK], start=True, stop=True)
                        last.then_inc(e_product, 1)
                    each_block(pe, i, one_block)
                each_dense_tile(pe, products)


_INS = ["x", "adj", "L0_gnn_w_self", "L0_gnn_w_neigh", "L1_gnn_W", "L1_gnn_a_l", "L1_gnn_a_r"]


def kernel(**inputs):
    import numpy as _np
    import concourse.bacc as _bacc
    from concourse import mybir as _mybir
    from concourse.bass_utils import run_bass_kernel_spmd as _run

    nc = _bacc.Bacc("TRN2", target_bir_lowering=False, num_devices=1)
    arrays, args = {}, []
    for name in _INS:
        a = _np.ascontiguousarray(inputs[name])
        arrays[f"in_{name}_dram"] = a
        args.append(nc.dram_tensor(f"in_{name}_dram", a.shape, _mybir.dt.from_np(a.dtype), kind="ExternalInput").ap())
    args.append(nc.dram_tensor("out_0_dram", inputs["x"].shape, _mybir.dt.float32, kind="ExternalOutput").ap())
    preln_gnn_gat_kernel(nc, *args)
    r = _run(nc, [arrays], core_ids=[0])
    return r.results[0]["out_0_dram"]
```

```python
from contextlib import ExitStack

import concourse.bass as bass
from concourse import mybir
import numpy as np

F32 = mybir.dt.float32
I32 = mybir.dt.int32
U32 = mybir.dt.uint32
ALU = mybir.AluOpType
ACT = mybir.ActivationFunctionType
AX = mybir.AxisListType

P = 128
EPS = 1e-5
SLOPE = 0.2
RING = 3
RING2 = 4
PEELED = 3
SENT = 8
SLOTS = 16
ALWAYS = 6
CAND = SLOTS + 1
LIGHT = 4
ABSENT = 65536.0
FAR = 1e30


def preln_gnn_gat_kernel(nc, x, adj, w_self, w_neigh, w_gat, a_l, a_r, out):
    N, D = x.shape
    HEADS, DK = a_l.shape
    TILES = N // P
    HALF = N // 2
    DC = D // P
    ROW = D + 2 * HEADS
    SR, SL = D, D + HEADS
    XCH = 8
    assert D == 2 * P and HEADS * DK == D
    SORT, UPD, SCORE, MIX = 4, 2, 4, 4
    KEY0 = HALF - 0.5
    OVF, SORTED = 7, 23
    KEYS = SORTED + SLOTS
    PACKED = LIGHT + 1
    EMPTY = KEY0 + 0.5 - N

    h0_dram = nc.dram_tensor("h0_table", [N, 1], F32, kind="Internal").ap()
    keys_dram = nc.dram_tensor("keys_table", [N, SLOTS], F32, kind="Internal").ap()
    row_dram = nc.dram_tensor("row_table", [N, ROW], F32, kind="Internal").ap()
    x_tiles = x.rearrange("(t p) d -> p t d", p=P)

    with ExitStack() as ctx:
        def sb(name, shape, dt=F32):
            return ctx.enter_context(nc.sbuf_tensor(name, shape, dt))

        def ps(name):
            return ctx.enter_context(nc.psum_tensor(name, [P, 512], F32))

        def sem(name):
            return ctx.enter_context(nc.semaphore(name))

        def ring(name, shape, dt=F32, depth=RING):
            return [sb(f"{name}{i}", shape, dt) for i in range(depth)]

        big = sb("big", [P, 2 * RING * (HALF + SENT)], I32)
        A = [big[:, s * (HALF + SENT):(s + 1) * (HALF + SENT)] for s in range(2 * RING)]
        bigf = big[:].bitcast(F32)
        used = [0]

        def of_big(*shape):
            width = int(np.prod(shape))
            used[0] += width
            part = bigf[:, used[0] - width:used[0]]
            return part.rearrange("p (a b) -> p a b", b=shape[1]) if len(shape) > 1 else part
        G = [of_big(PACKED, ROW) for _ in range(RING2)]
        at = (2 * RING - 1) * (HALF + SENT)
        w_raw, wn_raw, wneighT = (bigf[:, at + i * DC * D:at + (i + 1) * DC * D].rearrange("p (c d) -> p c d", c=DC)
                                  for i in range(3))
        al_b, ar_b, wa_tmp = (bigf[:, at + (3 * DC + i) * D:at + (3 * DC + i + 1) * D] for i in range(3))

        X = sb("x_rows", [P, TILES, D])
        keys_all = sb("keys_all", [P, TILES, SLOTS])
        stat0 = sb("stat0", [P, TILES, 6])
        mean0 = sb("mean0", [P, TILES])
        rstd0 = sb("rstd0", [P, TILES])
        nmr0 = sb("nmr0", [P, TILES])
        tmp0 = sb("tmp0", [P, TILES])
        h0c = sb("h0_columns", [P, TILES])
        h0r = sb("h0_rows", [TILES, P])
        ident = sb("ident", [P, P])
        ones = sb("ones", [P, P])
        eps = sb("eps", [P, 1])
        due_bias = sb("due_bias", [P, 1])
        find8 = sb("find8", [P, 8])
        rown = sb("rown", [P, TILES])
        wselfT = sb("wselfT", [P, DC, D])
        wx = sb("w_gat_and_heads", [P, DC, ROW])
        vsum = sb("w_neigh_sums", [P, D])
        mcol = sb("mcol", [P, P])
        tile_no = sb("tile_no", [1, TILES])
        listed = sb("listed", [1, TILES])
        listed2 = sb("listed2", [1, TILES])
        order = sb("order", [1, TILES])
        dense_tile = sb("dense_tile", [1, TILES], I32)
        dense_sum = sb("dense_sum", [1, 1])
        dense_count = sb("dense_count", [1, 1], I32)
        over = sb("over", [1, TILES, 2])
        degree = sb("degree", [1, TILES])
        more = sb("more", [1, TILES])
        due = sb("due", [1, TILES], I32)

        found = ring("found", [P, SLOTS], U32)
        keys = ring("keys", [P, KEYS])
        near_half = ring("near_half", [P, 8])
        rest = ring("rest", [P, SLOTS])
        valid = ring("valid", [P, KEYS])
        nbr = ring("nbr", [P, SLOTS], U32)
        h0g = ring("h0g", [P, SLOTS])
        svec = ring("s", [P, 1])
        junk = sb("junk", [P, SLOTS])
        junk1 = sb("junk1", [1, SLOTS])
        sdiag = ring("sdiag", [P, P])
        h = ring("h", [P, D])
        hT = ring("hT", [P, D])
        y = ring("low", [P, D])
        g = ring("g", [P, D])
        gT = ring("gT", [P, D])
        st1 = ring("st1_", [P, 6])
        mv1 = ring("mv1_", [P, 2])
        sd1 = ring("sd1_", [P, 1])
        rs1 = ring("rs1_", [P, 1])
        nm1 = ring("nm1_", [P, 1])
        rows = ring("rows", [P, ROW])
        nbr_last = sb("nbr_last", [P, SLOTS], U32)
        sc = ring("scores", [P, PACKED, HEADS], depth=RING2)
        sc2 = ring("leaky", [P, PACKED, HEADS], depth=RING2)
        mx = ring("mx", [P, HEADS], depth=RING2)
        pr = ring("probs", [P, PACKED, HEADS], depth=RING2)
        den = ring("den", [P, HEADS], depth=RING2)
        rden = ring("rden", [P, HEADS], depth=RING2)
        light = sb("light", [P, TILES])
        minus_ident = sb("minus_ident", [P, P])
        heavy_id = [sb(f"heavy_id{q}", [P, 1], U32) for q in range(2)]
        heavy_lists = [sb(f"heavy_lists{q}", [P, SLOTS], U32) for q in range(2)]
        heavy_pairs = sb("heavy_pairs", [1, 1], I32)
        most_due = sb("most_due", [1, 1], I32)

        p_u = [ps(f"p_u{i}") for i in range(RING)]
        p_hT, p_gT, p_row, p_cnt = ps("p_hT"), ps("p_gT"), ps("p_row"), ps("p_cnt")

        x_in = [sem(f"x_in{i}") for i in range(TILES // XCH)]
        w_in = sem("w_in")
        adj_in = [sem(f"adj_in{i}") for i in range(2 * RING)]
        sentinels = sem("sentinels")
        consts = sem("consts")
        pool_consts = sem("pool_consts")
        stat0_done, ln0_step, sd0_done, h0_done = sem("stat0_done"), sem("ln0_step"), sem("sd0_done"), sem("h0_done")
        h0_turned, h0_copied, h0_out = sem("h0_turned"), sem("h0_copied"), sem("h0_out")
        w_turned, w_copied, wa_step = sem("w_turned"), sem("w_copied"), sem("wa_step")
        vs_done, vs_copied = sem("vs_done"), sem("vs_copied")
        searched, keys_ready, sort_step, nbr_ready = sem("searched"), sem("keys_ready"), sem("sort_step"), sem("nbr_ready")
        valid_ready, counted = sem("valid_ready"), sem("counted")
        more_ready, due_ready = sem("more_ready"), sem("due_ready")
        count_copied, keys_kept, h0g_clear = sem("count_copied"), sem("keys_kept"), sem("h0g_clear")
        s_summed, sdiag_ready = sem("s_summed"), sem("sdiag_ready")
        h0_in = [sem(f"h0_in{i}") for i in range(RING)]
        h_ready, h_turned, hT_ready, u_ready = sem("h_ready"), sem("h_turned"), sem("hT_ready"), sem("u_ready")
        upd_step, mv_ready, sd_ready = sem("upd_step"), sem("mv_ready"), sem("sd_ready")
        rs_ready, norm_ready = sem("rs_ready"), sem("norm_ready")
        g_ready, g_turned, gT_ready = sem("g_ready"), sem("g_turned"), sem("gT_ready")
        row_ready, row_copied = sem("row_ready"), sem("row_copied")
        row_out = [sem(f"row_out{i}") for i in range(RING)]

        def wait_alone(eng, sem, value):
            if not isinstance(value, int):
                value = eng.to_reg(value)
                eng.wait_ge(consts, 1)
            eng.wait_ge(sem, value)

        def steps(depth):
            rounds = TILES // depth

            def num(k, r):
                return k * depth + r

            def later_round(k):
                return not isinstance(k, int) or k > 0

            def run(eng, *stages):
                def step(k, r):
                    for stage, lag in stages:
                        if not isinstance(k, int) or 0 <= num(k, r) - lag < TILES:
                            stage(k + (r - lag) // depth, (r - lag) % depth)
                for k in range(PEELED):
                    for r in range(depth):
                        step(k, r)
                with eng.Fori(PEELED, rounds) as k:
                    for r in range(depth):
                        step(k, r)
                for t in range(depth * rounds, TILES + max(lag for _, lag in stages)):
                    step(t // depth, t % depth)
            return num, later_round, run
        num, later_round, run = steps(RING)

        def due_of_tile(eng, k, r):
            return eng.value_load(due[0:1, bass.ds(num(k, r), 1)], min_val=16 * ALWAYS, max_val=16 * SLOTS)

        def ask_filled(pool, ask, tile_due, j=ALWAYS):
            if j < SLOTS:
                with pool.If(tile_due > 16 * j):
                    ask(j)
                    ask_filled(pool, ask, tile_due, j + 1)

        def x_tile(k, r):
            return X[:, bass.ds(num(k, r), 1), :].rearrange("p a d -> p (a d)")

        with nc.Block() as block:

            @block.sync
            def _(sp):
                for c in range(TILES // XCH):
                    sp.dma_start(X[:, c * XCH:(c + 1) * XCH, :], x_tiles[:, c * XCH:(c + 1) * XCH, :]
                                 ).then_inc(x_in[c], 16)

                def load(k, r):
                    for s in range(2):
                        if later_round(k):
                            sp.wait_ge(searched, num(k, r) * 2 + s + 1 - 2 * RING)
                        elif r == 1 and s == 0:
                            sp.wait_ge(h0_copied, 1)
                        elif r == RING - 1 and s == 1:
                            sp.wait_ge(vs_copied, 1)
                            sp.wait_ge(w_copied, 2)
                            sp.wait_ge(wa_step, 4 * DC)
                        b = 2 * r + s
                        sp.dma_start(A[b][:, 0:HALF], adj[bass.ds(num(k, r) * P, P), s * HALF:(s + 1) * HALF]
                                     ).then_inc(adj_in[b], 16)
                run(sp, (load, 0))

            @block.gpsimd
            def _(pool):
                nc.gpsimd.memset(ident[:], 0.0).then_inc(pool_consts, 1)
                nc.gpsimd.iota(rown[:], [[-P, TILES]], base=0, channel_multiplier=-1,
                               allow_small_or_imprecise_dtypes=True).then_inc(pool_consts, 1)
                nc.gpsimd.iota(mcol[:], [[1, P]], base=0, channel_multiplier=0,
                               allow_small_or_imprecise_dtypes=True).then_inc(pool_consts, 1)
                pool.wait_ge(pool_consts, 3)
                nc.gpsimd.affine_select(out=ident[:], in_=ident[:], compare_op=ALU.not_equal, fill=1.0,
                                        base=0, pattern=[[-1, P]], channel_multiplier=1).then_inc(pool_consts, 1)
                nc.gpsimd.tensor_scalar(rown[:], rown[:], KEY0, 1.0, ALU.add, ALU.mult).then_inc(pool_consts, 1)
                pool.wait_ge(h0_out, 16)
                def gather(k, r):
                    t = num(k, r)
                    wait_alone(pool, sort_step, (t + 1) * SORT)
                    if later_round(k):
                        wait_alone(pool, counted, t - RING + 1)
                        wait_alone(pool, s_summed, t - RING + 1)
                    nc.gpsimd.tensor_scalar(valid[r][:], keys[r][:], EMPTY, 1.0, ALU.is_ge, ALU.mult
                                            ).then_inc(valid_ready, 1)
                    nc.gpsimd.memset(h0g[r][:], 0.0).then_inc(h0g_clear, 1)
                    wait_alone(pool, h0g_clear, t + 1)
                    wait_alone(pool, nbr_ready, t + 1)
                    def ask(j):
                        nc.gpsimd.indirect_dma_start(
                            out=h0g[r][:, j:j + 1], out_offset=None, in_=h0_dram[:, :],
                            in_offset=bass.IndirectOffsetOnAxis(ap=nbr[r][:, j:j + 1], axis=0),
                            bounds_check=N - 1, oob_is_err=False).then_inc(h0_in[r], 16)
                    for j in range(ALWAYS):
                        ask(j)
                    wait_alone(pool, due_ready, t + 1)
                    ask_filled(pool, ask, due_of_tile(pool, k, r))
                run(pool, (gather, 0))

            @block.vector
            def _(dve):
                for b in A:
                    nc.vector.memset(b[:, HALF:HALF + SENT], 1).then_inc(sentinels, 1)
                nc.vector.memset(find8[:], 1.0)
                nc.vector.memset(eps[:], EPS)
                nc.vector.memset(due_bias[:], -16.0 * ALWAYS)
                for b in keys:
                    nc.vector.memset(b[:], 0.0)
                nc.vector.memset(ones[:], 1.0).then_inc(consts, 1)

                for c in range(TILES // XCH):
                    dve.wait_ge(x_in[c], 16)
                    for t in range(c * XCH, (c + 1) * XCH):
                        last = nc.vector.bn_stats(stat0[:, t, :], X[:, t, :])
                last.then_inc(stat0_done, 1)
                dve.wait_ge(stat0_done, 1)

                def ln(ins, n):
                    ins.then_inc(ln0_step, 1)
                    dve.wait_ge(ln0_step, n)
                nc.vector.tensor_tensor(mean0[:], stat0[:, :, 1], stat0[:, :, 4], ALU.add)
                nc.vector.tensor_tensor(tmp0[:], stat0[:, :, 1], stat0[:, :, 4], ALU.subtract)
                ln(nc.vector.tensor_tensor(nmr0[:], stat0[:, :, 2], stat0[:, :, 5], ALU.add), 1)
                nc.vector.tensor_scalar(mean0[:], mean0[:], -0.5, None, ALU.mult)
                ln(nc.vector.tensor_tensor(tmp0[:], tmp0[:], tmp0[:], ALU.mult), 2)
                ln(nc.vector.scalar_tensor_tensor(tmp0[:], tmp0[:], D / 4.0, nmr0[:], ALU.mult, ALU.add), 3)
                dve.wait_ge(sd0_done, 1)
                ln(nc.vector.reciprocal(rstd0[:], tmp0[:]), 4)
                nc.vector.tensor_tensor(nmr0[:], mean0[:], rstd0[:], ALU.mult)
                ln(nc.vector.tensor_tensor(h0c[:], X[:, :, 0], rstd0[:], ALU.mult), 5)
                ln(nc.vector.tensor_tensor(h0c[:], h0c[:], nmr0[:], ALU.add), 6)
                nc.vector.tensor_scalar(h0c[:], h0c[:], 0.0, None, ALU.max).then_inc(h0_done, 1)

                dve.wait_ge(w_in, 16 * 5)
                dve.wait_ge(consts, 1)
                n = 0
                for c in range(DC):
                    for at_col, a in ((SR, ar_b), (SL, al_b)):
                        nc.vector.tensor_tensor(wa_tmp, wx[:, c, 0:D], a, ALU.mult).then_inc(wa_step, 1)
                        dve.wait_ge(wa_step, n + 1)
                        nc.vector.tensor_reduce(wx[:, c, at_col:at_col + HEADS],
                                                wa_tmp.rearrange("p (h k) -> p h k", h=HEADS), AX.X, ALU.add
                                                ).then_inc(wa_step, 1)
                        n += 2
                        dve.wait_ge(wa_step, n)

                def search(k, r, s):
                    if later_round(k):
                        wait_alone(dve, keys_ready, (num(k, r) - RING) * 2 + s + 1)
                    wait_alone(dve, adj_in[2 * r + s], k * 16 + 16)
                    nc.vector.max_index(found[r][:, 8 * s:8 * s + 8], find8[:], A[2 * r + s]).then_inc(searched, 1)

                def search_first(k, r):
                    search(k, r, 0)

                def search_second(k, r):
                    search(k, r, 1)

                def sort(k, r):
                    t = num(k, r)

                    def step(ins, n):
                        ins.then_inc(sort_step, 1)
                        if n < SORT:
                            wait_alone(dve, sort_step, t * SORT + n)
                    if later_round(k):
                        wait_alone(dve, keys_kept, t - RING + 1)
                        wait_alone(dve, valid_ready, t - RING + 1)
                    wait_alone(dve, keys_ready, 2 * t + 2)
                    step(nc.vector.scalar_tensor_tensor(keys[r][:, 0:8], near_half[r][:], ABSENT, near_half[r][:],
                                                        ALU.mult, ALU.min), 1)
                    step(nc.vector.max(keys[r][:, SORTED:SORTED + 8], keys[r][:, 0:SLOTS]), 2)
                    step(nc.vector.match_replace(rest[r][:], keys[r][:, SORTED:SORTED + 8], keys[r][:, 0:SLOTS], -1e9), 3)
                    step(nc.vector.max(keys[r][:, SORTED + 8:KEYS], rest[r][:]), 4)

                def update(k, r):
                    t = num(k, r)

                    def step(ins, n):
                        ins.then_inc(upd_step, 1)
                        wait_alone(dve, upd_step, t * UPD + n)
                    wait_alone(dve, u_ready, t + 1)
                    step(nc.vector.scalar_tensor_tensor(x_tile(k, r), p_u[r][:, 0:D], 0.0, x_tile(k, r), ALU.max, ALU.add), 1)
                    step(nc.vector.bn_stats(st1[r][:], x_tile(k, r)), 2)
                    if later_round(k):
                        wait_alone(dve, g_ready, t - RING + 1)
                    nc.vector.bn_aggr(mv1[r][:], st1[r][:]).then_inc(mv_ready, 1)

                def norm(k, r):
                    t = num(k, r)
                    dve.wait_ge(sd_ready, t + 1)
                    nc.vector.reciprocal(rs1[r][:], sd1[r][:]).then_inc(rs_ready, 1)
                    dve.wait_ge(rs_ready, t + 1)
                    nc.vector.scalar_tensor_tensor(nm1[r][:], mv1[r][:, 0:1], -1.0, rs1[r][:], ALU.mult, ALU.mult
                                                   ).then_inc(norm_ready, 1)
                run(dve, (search_first, 0), (sort, 1), (update, 3), (norm, 4), (search_second, 0))

            @block.scalar
            def _(act):
                act.dma_start(w_raw, w_self.rearrange("(c p) d -> p c d", p=P)).then_inc(w_in, 16)
                act.dma_start(wn_raw, w_neigh.rearrange("(c p) d -> p c d", p=P)).then_inc(w_in, 16)
                act.dma_start(wx[:, :, 0:D], w_gat.rearrange("(c p) d -> p c d", p=P)).then_inc(w_in, 16)
                act.dma_start(al_b, a_l.rearrange("(o h) k -> o (h k)", o=1).broadcast_to([P, D])).then_inc(w_in, 16)
                act.dma_start(ar_b, a_r.rearrange("(o h) k -> o (h k)", o=1).broadcast_to([P, D])).then_inc(w_in, 16)
                for i, dst in enumerate((wselfT[:], wneighT)):
                    act.wait_ge(w_turned, i + 1)
                    nc.scalar.copy(dst.rearrange("p c d -> p (c d)"), p_u[i][:]).then_inc(w_copied, 1)
                act.wait_ge(vs_done, 1)
                nc.scalar.copy(vsum[:], p_u[2][:, 0:D]).then_inc(vs_copied, 1)
                act.wait_ge(ln0_step, 3)
                nc.scalar.activation(tmp0[:], tmp0[:], ACT.Sqrt, bias=eps[:], scale=1.0 / D).then_inc(sd0_done, 1)
                act.wait_ge(h0_turned, 1)
                nc.scalar.copy(h0r[:], p_cnt[0:TILES, 0:P]).then_inc(h0_copied, 1)
                act.wait_ge(h0_copied, 1)
                act.dma_start(h0_dram.rearrange("(t p) o -> t (p o)", p=P), h0r[:]).then_inc(h0_out, 16)

                due_total = [act.alloc_register(f"h0_due_total{i}") for i in range(RING)]
                for r in range(RING):
                    act.reg_mov(due_total[r], 0)

                def make_keys(k, r):
                    t = num(k, r)
                    act.wait_ge(searched, 2 * t + 2)
                    if later_round(k):
                        act.wait_ge(sort_step, (t - RING + 1) * SORT)
                        act.wait_ge(valid_ready, t - RING + 1)
                    nc.scalar.activation(near_half[r][:], found[r][:, 0:8], ACT.Copy, bias=KEY0, scale=-1.0
                                         ).then_inc(keys_ready, 1)
                    nc.scalar.activation(keys[r][:, 8:16], found[r][:, 8:16], ACT.Copy, bias=KEY0 - HALF, scale=-1.0
                                         ).then_inc(keys_ready, 1)

                def list_neighbours(k, r):
                    t = num(k, r)
                    act.wait_ge(sort_step, (t + 1) * SORT)
                    if later_round(k):
                        act.wait_ge(s_summed, t - RING + 1)
                    sorted_keys = keys[r][:, SORTED:KEYS]
                    nc.scalar.activation(nbr[r][:], sorted_keys, ACT.Copy, bias=KEY0, scale=-1.0).then_inc(nbr_ready, 1)
                    nc.scalar.copy(keys_all[:, bass.ds(t, 1), :].rearrange("p a j -> p (a j)"), sorted_keys
                                   ).then_inc(keys_kept, 1)

                def keep_counts(k, r):
                    t = num(k, r)
                    act.wait_ge(counted, t + 1)
                    nc.scalar.activation(junk1[:], p_cnt[0:1, SORTED:KEYS], ACT.Sign, accum_out=degree[0:1, bass.ds(t, 1)]
                                         ).then_inc(count_copied, 1)
                    nc.scalar.copy(over[0:1, bass.ds(t, 1), :].rearrange("p a j -> p (a j)"), p_cnt[0:1, OVF:SLOTS:8]
                                   ).then_inc(count_copied, 1)
                    wait_alone(act, count_copied, 2 * t + 2)
                    nc.scalar.activation(more[0:1, bass.ds(t, 1)], degree[0:1, bass.ds(t, 1)], ACT.Relu,
                                         bias=due_bias[0:1, :], scale=16.0).then_inc(more_ready, 1)
                    act.wait_ge(more_ready, t + 1)
                    nc.scalar.activation(due[0:1, bass.ds(t, 1)], more[0:1, bass.ds(t, 1)], ACT.Copy, bias=16.0 * ALWAYS
                                         ).then_inc(due_ready, 1)

                def first_norm(k, r):
                    t = num(k, r)
                    if later_round(k):
                        wait_alone(act, h_turned, t - RING + 1)
                    nc.scalar.activation(h[r][:], x_tile(k, r), ACT.Relu, bias=nmr0[:, bass.ds(t, 1)],
                                         scale=rstd0[:, bass.ds(t, 1)]).then_inc(h_ready, 1)
                    act.wait_ge(h_turned, t + 1)
                    if later_round(k):
                        act.wait_ge(u_ready, t - RING + 1)
                    nc.scalar.copy(hT[r][:], p_hT[:, 0:D]).then_inc(hT_ready, 1)

                def sum_neighbours(k, r):
                    t = num(k, r)
                    wait_alone(act, due_ready, t + 1)
                    act.reg_add(due_total[r], due_total[r], due_of_tile(act, k, r))
                    act.wait_ge(h0_in[r], act.snap(due_total[r]))
                    nc.scalar.activation(junk[:], h0g[r][:], ACT.Copy, accum_out=svec[r][:]).then_inc(s_summed, 1)
                    act.wait_ge(s_summed, t + 1)
                    nc.scalar.activation(sdiag[r][:], ident[:], ACT.Copy, scale=svec[r][:]).then_inc(sdiag_ready, 1)

                def deviation(k, r):
                    act.wait_ge(mv_ready, num(k, r) + 1)
                    nc.scalar.activation(sd1[r][:], mv1[r][:, 1:2], ACT.Sqrt, bias=eps[:]).then_inc(sd_ready, 1)

                def second_norm(k, r):
                    t = num(k, r)
                    wait_alone(act, norm_ready, t + 1)
                    if later_round(k):
                        act.wait_ge(g_turned, t - RING + 1)
                    nc.scalar.activation(g[r][:], x_tile(k, r), ACT.Relu, bias=nm1[r][:], scale=rs1[r][:]
                                         ).then_inc(g_ready, 1)
                    act.wait_ge(g_turned, t + 1)
                    if later_round(k):
                        act.wait_ge(row_ready, t - RING + 1)
                    nc.scalar.copy(gT[r][:], p_gT[:, 0:D]).then_inc(gT_ready, 1)

                def write_rows(k, r):
                    t = num(k, r)
                    act.wait_ge(row_ready, t + 1)
                    if later_round(k):
                        act.wait_ge(row_out[r], k * 16)
                    nc.scalar.copy(rows[r][:], p_row[:, 0:ROW]).then_inc(row_copied, 1)
                    act.wait_ge(row_copied, t + 1)
                    act.dma_start(row_dram[bass.ds(t * P, P), :], rows[r][:]).then_inc(row_out[r], 16)
                run(act, (list_neighbours, 1), (keep_counts, 1), (first_norm, 2), (deviation, 3), (second_norm, 4),
                    (make_keys, 0), (sum_neighbours, 2), (write_rows, 4))
                for r in range(RING):
                    act.wait_ge(row_out[r], 16 * len(range(r, TILES, RING)))

            @block.tensor
            def _(pe):
                pe.wait_ge(w_in, 16 * 5)
                pe.wait_ge(pool_consts, 5)
                for i, raw in enumerate((w_raw, wn_raw)):
                    for c in range(DC):
                        for o in range(DC):
                            at_col = c * D + o * P
                            last = nc.tensor.transpose(p_u[i][:, at_col:at_col + P], raw[:, o, c * P:(c + 1) * P], ident[:])
                    last.then_inc(w_turned, 1)
                pe.wait_ge(w_copied, 2)
                pe.wait_ge(consts, 1)
                for c in range(DC):
                    last = nc.tensor.matmul(p_u[2][:, 0:D], ones[:], wneighT[:, c, :], start=(c == 0), stop=(c == DC - 1))
                last.then_inc(vs_done, 1)
                pe.wait_ge(h0_done, 1)
                nc.tensor.transpose(p_cnt[0:TILES, 0:P], h0c[:], ident[:]).then_inc(h0_turned, 1)
                pe.wait_ge(h0_copied, 1)
                pe.wait_ge(vs_copied, 1)
                pe.wait_ge(wa_step, 4 * DC)

                def count(k, r):
                    t = num(k, r)
                    pe.wait_ge(valid_ready, t + 1)
                    if not (isinstance(t, int) and t == 0):
                        pe.wait_ge(due_ready, t)
                    nc.tensor.matmul(p_cnt[:, 0:KEYS], ones[:], valid[r][:], start=True, stop=True).then_inc(counted, 1)

                def turn_first(k, r):
                    t = num(k, r)
                    pe.wait_ge(h_ready, t + 1)
                    if not (isinstance(t, int) and t == 0):
                        pe.wait_ge(hT_ready, t)
                    for c in range(DC):
                        last = nc.tensor.transpose(p_hT[:, c * P:(c + 1) * P], h[r][:, c * P:(c + 1) * P], ident[:])
                    last.then_inc(h_turned, 1)

                def first_product(k, r):
                    t = num(k, r)
                    pe.wait_ge(hT_ready, t + 1)
                    if later_round(k):
                        pe.wait_ge(upd_step, (t - RING) * UPD + 1)
                    for c in range(DC):
                        nc.tensor.matmul(p_u[r][:, 0:D], hT[r][:, c * P:(c + 1) * P], wselfT[:, c, :],
                                         start=(c == 0), stop=False)
                    pe.wait_ge(sdiag_ready, t + 1)
                    nc.tensor.matmul(p_u[r][:, 0:D], sdiag[r][:], vsum[:], start=False, stop=True).then_inc(u_ready, 1)

                def table_rows(k, r):
                    t = num(k, r)
                    pe.wait_ge(g_ready, t + 1)
                    if not (isinstance(t, int) and t == 0):
                        pe.wait_ge(gT_ready, t)
                    for c in range(DC):
                        last = nc.tensor.transpose(p_gT[:, c * P:(c + 1) * P], g[r][:, c * P:(c + 1) * P], ident[:])
                    last.then_inc(g_turned, 1)
                    pe.wait_ge(gT_ready, t + 1)
                    if not (isinstance(t, int) and t == 0):
                        pe.wait_ge(row_copied, t)
                    for c in range(DC):
                        last = nc.tensor.matmul(p_row[:, 0:ROW], gT[r][:, c * P:(c + 1) * P], wx[:, c, :],
                                                start=(c == 0), stop=(c == DC - 1))
                    last.then_inc(row_ready, 1)
                run(pe, (count, 1), (turn_first, 2), (table_rows, 4), (first_product, 2))

        tiles_listed, list_step = sem("tiles_listed"), sem("list_step")
        d_free, d_in, d_h, d_hT, d_hT_copied, d_u = (sem(f"d_{n}") for n in ("free", "in", "h", "hT", "hT_copied", "u"))
        d_step, d_stats, d_sd, d_norm = (sem(f"d_{n}") for n in ("step", "stats", "sd", "norm"))
        d_g, d_gT, d_gT_copied, d_row, d_row_copied, d_out = (
            sem(f"d_{n}") for n in ("g", "gT", "gT_copied", "row", "row_copied", "out"))
        D_STEPS = 7
        h0_all = [bigf[:, (2 + s) * (HALF + SENT):(2 + s) * (HALF + SENT) + HALF] for s in range(2)]
        part = sb("part", [P, 2])

        def each_dense_tile(eng, body):
            eng.wait_ge(tiles_listed, 1)
            count = eng.value_load(dense_count[0:1, 0:1], min_val=0, max_val=TILES)
            with eng.If(count > 0):
                with eng.Fori(0, count) as i:
                    body(i, eng.value_load(dense_tile[0:1, bass.ds(i, 1)], min_val=0, max_val=TILES - 1))
                eng.wait_ge(tiles_listed, 1)

        def x_at(t):
            return X[:, bass.ds(t, 1), :].rearrange("p a d -> p (a d)")

        with nc.Block() as block:

            @block.sync
            def _(sp):
                def load(i, t):
                    sp.wait_ge(d_free, i + 1)
                    sp.dma_start(x_at(t), x[bass.ds(t * P, P), :]).then_inc(d_in, 16)
                    for s in range(2):
                        sp.dma_start(A[s][:, 0:HALF], adj[bass.ds(t * P, P), s * HALF:(s + 1) * HALF]).then_inc(d_in, 16)
                        sp.dma_start(h0_all[s], h0_dram[s * HALF:(s + 1) * HALF, :].rearrange("n o -> o n")
                                     .broadcast_to([P, HALF])).then_inc(d_in, 16)
                each_dense_tile(sp, load)

            @block.vector
            def _(dve):
                def step(ins, n):
                    ins.then_inc(list_step, 1)
                    dve.wait_ge(list_step, n)
                step(nc.vector.tensor_tensor(listed[:], over[:, :, 0], over[:, :, 1], ALU.add), 1)
                step(nc.vector.tensor_scalar(listed2[:], listed[:], 0.5, None, ALU.is_gt), 2)
                step(nc.vector.tensor_reduce(dense_sum[:], listed2[:], AX.X, ALU.add), 3)
                step(nc.vector.tensor_copy(dense_count[:], dense_sum[:]), 4)
                with dve.If(dve.value_load(dense_count[0:1, 0:1], min_val=0, max_val=TILES) > 0):
                    step(nc.vector.tensor_scalar(tile_no[:], rown[0:1, :], -1.0 / P, KEY0 / P + 1.0, ALU.mult, ALU.add), 5)
                    step(nc.vector.tensor_tensor(listed[:], listed2[:], tile_no[:], ALU.mult), 6)
                    n, src, dst = 6, listed, listed2
                    for c in range(TILES // 8):
                        step(nc.vector.max(order[:, 8 * c:8 * c + 8], src[:]), n + 1)
                        step(nc.vector.match_replace(dst[:], order[:, 8 * c:8 * c + 8], src[:], -1.0), n + 2)
                        n, src, dst = n + 2, dst, src
                    step(nc.vector.tensor_scalar(dense_tile[:], order[:], -1.0, 0.0, ALU.add, ALU.max), n + 1)
                dve.sem_inc(tiles_listed, 1)
                dve.sem_inc(d_free, 1)

                def sums(i, t):
                    def step(ins, n):
                        ins.then_inc(d_step, 1)
                        wait_alone(dve, d_step, i * D_STEPS + n)
                    dve.wait_ge(d_in, (i + 1) * 16 * 5)
                    for s in range(2):
                        step(nc.vector.tensor_tensor_reduce(h0_all[s], A[s][:, 0:HALF], h0_all[s], 1.0, 0.0,
                                                            ALU.mult, ALU.add, part[:, s:s + 1]), s + 1)
                    step(nc.vector.tensor_tensor(svec[0][:], part[:, 0:1], part[:, 1:2], ALU.add), 3)
                    dve.wait_ge(d_u, i + 1)
                    step(nc.vector.scalar_tensor_tensor(y[0][:], vsum[:], svec[0][:], p_u[0][:, 0:D], ALU.mult, ALU.add), 4)
                    step(nc.vector.scalar_tensor_tensor(x_at(t), y[0][:], 0.0, x_at(t), ALU.max, ALU.add), 5)
                    step(nc.vector.bn_stats(st1[0][:], x_at(t)), 6)
                    nc.vector.bn_aggr(mv1[0][:], st1[0][:]).then_inc(d_stats, 1)
                    dve.wait_ge(d_sd, i + 1)
                    step(nc.vector.reciprocal(rs1[0][:], sd1[0][:]), 7)
                    nc.vector.scalar_tensor_tensor(nm1[0][:], mv1[0][:, 0:1], -1.0, rs1[0][:], ALU.mult, ALU.mult
                                                   ).then_inc(d_norm, 1)
                each_dense_tile(dve, sums)

            @block.scalar
            def _(act):
                def norms(i, t):
                    wait_alone(act, d_in, (i + 1) * 16 * 5)
                    nc.scalar.activation(h[0][:], x_at(t), ACT.Relu, bias=nmr0[:, bass.ds(t, 1)],
                                         scale=rstd0[:, bass.ds(t, 1)]).then_inc(d_h, 1)
                    act.wait_ge(d_hT, i + 1)
                    nc.scalar.copy(hT[0][:], p_hT[:, 0:D]).then_inc(d_hT_copied, 1)
                    act.wait_ge(d_stats, i + 1)
                    nc.scalar.activation(sd1[0][:], mv1[0][:, 1:2], ACT.Sqrt, bias=eps[:]).then_inc(d_sd, 1)
                    wait_alone(act, d_norm, i + 1)
                    nc.scalar.activation(g[0][:], x_at(t), ACT.Relu, bias=nm1[0][:], scale=rs1[0][:]).then_inc(d_g, 1)
                    act.wait_ge(d_gT, i + 1)
                    nc.scalar.copy(gT[0][:], p_gT[:, 0:D]).then_inc(d_gT_copied, 1)
                    act.wait_ge(d_row, i + 1)
                    nc.scalar.copy(rows[0][:], p_row[:, 0:ROW]).then_inc(d_row_copied, 1)
                    act.wait_ge(d_row_copied, i + 1)
                    act.dma_start(row_dram[bass.ds(t * P, P), :], rows[0][:]).then_inc(d_out, 16)
                    act.wait_ge(d_out, (i + 1) * 16)
                    act.sem_inc(d_free, 1)
                each_dense_tile(act, norms)

            @block.tensor
            def _(pe):
                def products(i, t):
                    pe.wait_ge(d_h, i + 1)
                    for c in range(DC):
                        last = nc.tensor.transpose(p_hT[:, c * P:(c + 1) * P], h[0][:, c * P:(c + 1) * P], ident[:])
                    last.then_inc(d_hT, 1)
                    pe.wait_ge(d_hT_copied, i + 1)
                    for c in range(DC):
                        last = nc.tensor.matmul(p_u[0][:, 0:D], hT[0][:, c * P:(c + 1) * P], wselfT[:, c, :],
                                                start=(c == 0), stop=(c == DC - 1))
                    last.then_inc(d_u, 1)
                    pe.wait_ge(d_g, i + 1)
                    for c in range(DC):
                        last = nc.tensor.transpose(p_gT[:, c * P:(c + 1) * P], g[0][:, c * P:(c + 1) * P], ident[:])
                    last.then_inc(d_gT, 1)
                    pe.wait_ge(d_gT_copied, i + 1)
                    for c in range(DC):
                        last = nc.tensor.matmul(p_row[:, 0:ROW], gT[0][:, c * P:(c + 1) * P], wx[:, c, :],
                                                start=(c == 0), stop=(c == DC - 1))
                    last.then_inc(d_row, 1)
                each_dense_tile(pe, products)

        table_step, pack_step = sem("table_step"), sem("pack_step")
        tiles_counted, counts_copied, ranked, packed = sem("tiles_counted"), sem("counts_copied"), sem("ranked"), sem("packed")
        spread, pack_ready, keys_out = sem("spread"), sem("pack_ready"), sem("keys_out")
        lists_ready, self_in = sem("lists_ready"), [sem(f"self_in{i}") for i in range(RING2)]
        rows_in = [sem(f"rows_in{i}") for i in range(RING2)]
        score_step, shifted, exp_done = sem("score_step"), sem("shifted"), sem("exp_done")
        mix_step, mixed, mixed_exp, parts_ready = sem("mix_step"), sem("mixed"), sem("mixed_exp"), sem("parts_ready")
        elu_ready, res_ready = sem("elu_ready"), sem("res_ready")
        p_elu = p_u + [p_hT]
        res_out = [sem(f"res_out{i}") for i in range(RING2)]
        lists, mixv, low, res = nbr + [nbr_last], h + hT[0:1], y + hT[1:2], g + hT[2:3]
        num, later_round, run = steps(RING2)
        w_keys_in, w_rows_in, w_x_in, w_out = ([sem(f"{n}{q}") for q in range(2)]
                                               for n in ("w_keys_in", "w_rows_in", "w_x_in", "w_out"))
        tri_step, w_lists_ready, w_step = (sem(n) for n in ("tri_step", "w_lists_ready", "w_step"))
        w_ids_free, w_ids_ready = sem("w_ids_free"), sem("w_ids_ready")
        w_shifted, w_exp_done, w_mixed, w_mixed_exp, w_low_ready, w_res_ready = (
            sem(f"w_{n}") for n in ("shifted", "exp_done", "mixed", "mixed_exp", "low_ready", "res_ready"))
        HEAVY_STEPS = 11
        NAMED = 8
        ROUND = 1.5 * 2 ** 23
        pairs, heavy, row_number, place, block_no, place_in, id_key = (of_big(TILES) for _ in range(7))
        idf = of_big(TILES + 2)
        penalty = of_big(TILES, PACKED)
        gone = of_big(TILES, LIGHT)
        earlier, tiles_before = of_big(P), of_big(P)
        hot_start = used[0]
        hot_place, hot_block = of_big(TILES, P), of_big(TILES, TILES)
        used[0] = hot_start
        HG = [of_big(CAND, ROW) for _ in range(2)]
        w_x, w_mix, w_low, w_res = ([of_big(D) for _ in range(2)] for _ in range(4))
        w_keys, w_gone = ([of_big(SLOTS) for _ in range(2)] for _ in range(2))
        w_penalty = [of_big(CAND) for _ in range(2)]
        w_sc, w_sc2, w_pr = ([of_big(CAND, HEADS) for _ in range(2)] for _ in range(3))
        w_mx, w_den, w_rden = ([of_big(HEADS) for _ in range(2)] for _ in range(3))

        def heads(ap, n):
            return ap.rearrange("p (o h) -> p o h", o=1).broadcast_to([P, n, HEADS])

        def slots_first(ap):
            return ap.rearrange("p j h -> p h j")

        def each_heavy_pair(eng, body):
            wait_alone(eng, pack_ready, 2)
            count = eng.value_load(heavy_pairs[0:1, 0:1], min_val=0, max_val=TILES // 2)
            with eng.If(count > 0):
                with eng.Fori(0, count) as i:
                    body(i)

        with nc.Block() as block:

            @block.sync
            def _(sp):
                sp.dma_start(keys_dram.rearrange("(t p) j -> p t j", p=P), keys_all[:]).then_inc(keys_out, 16)

                def own_rows(k, r):
                    t = num(k, r)
                    if later_round(k):
                        sp.wait_ge(mixed, t - RING2 + 1)
                    sp.dma_start(G[r][:, 0, :], row_dram[bass.ds(t * P, P), :]).then_inc(self_in[r], 16)

                def write(k, r):
                    t = num(k, r)
                    sp.wait_ge(res_ready, t + 1)
                    sp.dma_start(out[bass.ds(t * P, P), :], res[r][:]).then_inc(res_out[r], 16)
                run(sp, (own_rows, 0), (write, 5))
                sp.wait_ge(keys_out, 16)
                for r in range(RING2):
                    sp.wait_ge(res_out[r], 16 * len(range(r, TILES, RING2)))

            @block.gpsimd
            def _(pool):
                nc.gpsimd.memset(earlier, 1.0).then_inc(tri_step, 1)
                pool.wait_ge(tri_step, 1)
                nc.gpsimd.affine_select(out=earlier, in_=earlier, compare_op=ALU.is_gt, fill=0.0,
                                        base=0, pattern=[[1, P]], channel_multiplier=-1).then_inc(tri_step, 1)

                def gather(k, r):
                    t = num(k, r)
                    wait_alone(pool, lists_ready, t + 1)
                    if later_round(k):
                        wait_alone(pool, mixed, t - RING2 + 1)
                    for j in range(LIGHT):
                        nc.gpsimd.indirect_dma_start(
                            out=G[r][:, j + 1, :], out_offset=None, in_=row_dram[:, :],
                            in_offset=bass.IndirectOffsetOnAxis(ap=lists[r][:, j:j + 1], axis=0),
                            bounds_check=N - 1, oob_is_err=False).then_inc(rows_in[r], 16)
                run(pool, (gather, 0))
                pool.wait_ge(keys_out, 16)

                def from_table(table, dst, ids, signal):
                    nc.gpsimd.indirect_dma_start(
                        out=dst, out_offset=None, in_=table[:, :], in_offset=bass.IndirectOffsetOnAxis(ap=ids, axis=0),
                        bounds_check=N - 1, oob_is_err=False).then_inc(signal, 16)

                def heavy_pair(i):
                    wait_alone(pool, w_ids_ready, i * 2 + 2)
                    for q in range(2):
                        from_table(keys_dram, w_keys[q], heavy_id[q][:], w_keys_in[q])
                        from_table(row_dram, HG[q][:, 0, :], heavy_id[q][:], w_rows_in[q])
                    most = pool.value_load(most_due[0:1, 0:1], min_val=16 * ALWAYS, max_val=16 * SLOTS)
                    for q in range(2):
                        wait_alone(pool, w_keys_in[q], (i + 1) * 16)
                        nc.gpsimd.tensor_scalar(heavy_lists[q][:], w_keys[q], -1.0, KEY0, ALU.mult, ALU.add
                                                ).then_inc(w_lists_ready, 1)
                        wait_alone(pool, w_lists_ready, i * 2 + q + 1)

                        def ask(j):
                            from_table(row_dram, HG[q][:, j + 1, :], heavy_lists[q][:, j:j + 1], w_rows_in[q])
                        for j in range(ALWAYS):
                            ask(j)
                        ask_filled(pool, ask, most)
                    for r in range(RING2):
                        pool.wait_ge(res_out[r], 16 * len(range(r, TILES, RING2)))
                    for q in range(2):
                        from_table(out, w_x[q], heavy_id[q][:], w_x_in[q])
                    for q in range(2):
                        wait_alone(pool, w_res_ready, i * 2 + q + 1)
                        nc.gpsimd.indirect_dma_start(
                            out=out[:, :], out_offset=bass.IndirectOffsetOnAxis(ap=heavy_id[q][:], axis=0), in_=w_res[q],
                            in_offset=None, bounds_check=N - 1, oob_is_err=False).then_inc(w_out[q], 16)
                    for q in range(2):
                        wait_alone(pool, w_out[q], (i + 1) * 16)
                    pool.sem_inc(w_ids_free, 1)
                each_heavy_pair(pool, heavy_pair)

            @block.tensor
            def _(pe):
                pe.wait_ge(pack_step, 1)
                nc.tensor.matmul(p_hT[0:TILES, 0:P], heavy, ones[:], start=True, stop=True).then_inc(tiles_counted, 1)
                pe.wait_ge(tri_step, 2)
                nc.tensor.matmul(p_gT[:, 0:TILES], earlier, heavy, start=True, stop=False)
                pe.wait_ge(counts_copied, 1)
                nc.tensor.matmul(p_gT[:, 0:TILES], tiles_before[0:TILES, :], earlier[0:TILES, 0:TILES],
                                 start=False, stop=True).then_inc(ranked, 1)
                nc.tensor.matmul(p_cnt[:, 0:TILES], ones[:], heavy, start=True, stop=True).then_inc(ranked, 1)

                def pack_rows(k, r):
                    if not isinstance(k, int) or num(k, r) >= NAMED:
                        return
                    share = TILES // NAMED
                    if num(k, r) == 0:
                        pe.wait_ge(spread, 1)
                    for t in range(num(k, r) * share, (num(k, r) + 1) * share):
                        last = nc.tensor.matmul(p_row[:, 0:TILES], hot_place[:, t, :], hot_block[:, t, :],
                                                start=(t == 0), stop=(t == TILES - 1))
                    if num(k, r) == NAMED - 1:
                        last.then_inc(packed, 1)

                def add_parts(k, r):
                    t = num(k, r)
                    pe.wait_ge(parts_ready, t + 1)
                    if later_round(k):
                        pe.wait_ge(res_ready, t - RING2 + 1)
                    nc.tensor.matmul(p_elu[r][:, 0:D], ident[:], mixv[r][:], start=True, stop=False)
                    nc.tensor.matmul(p_elu[r][:, 0:D], minus_ident[:], low[r][:], start=False, stop=True
                                     ).then_inc(elu_ready, 1)
                run(pe, (pack_rows, 0), (add_parts, 0))

            @block.scalar
            def _(act):
                act.wait_ge(tiles_counted, 1)
                nc.scalar.copy(tiles_before[0:TILES, :], p_hT[0:TILES, 0:P]).then_inc(counts_copied, 1)

                def list_rows(k, r):
                    t = num(k, r)
                    if later_round(k):
                        act.wait_ge(mixed, t - RING2 + 1)
                    nc.scalar.activation(lists[r][:], keys_all[:, bass.ds(t, 1), :].rearrange("p a j -> p (a j)"),
                                         ACT.Copy, bias=KEY0, scale=-1.0).then_inc(lists_ready, 1)

                def exps(k, r):
                    act.wait_ge(shifted, num(k, r) + 1)
                    nc.scalar.activation(pr[r][:], sc[r][:], ACT.Exp).then_inc(exp_done, 1)

                def elu_parts(k, r):
                    t = num(k, r)
                    wait_alone(act, mixed, t + 1)
                    if later_round(k):
                        wait_alone(act, res_ready, t - RING2 + 1)
                    nc.scalar.activation(low[r][:], mixv[r][:], ACT.Exp, scale=light[:, bass.ds(t, 1)]).then_inc(mixed_exp, 1)
                    wait_alone(act, mixed_exp, t + 1)
                    nc.scalar.activation(mixv[r][:], mixv[r][:], ACT.Relu, scale=light[:, bass.ds(t, 1)])
                    nc.scalar.activation(low[r][:], low[r][:], ACT.Relu, bias=1.0, scale=-1.0).then_inc(parts_ready, 1)

                def first_ids(k, r):
                    if isinstance(k, int) and num(k, r) == PEELED * RING2 - 1:
                        act.wait_ge(pack_ready, 2)
                        for q in range(2):
                            nc.scalar.activation(heavy_id[q][:], idf[:, q:q + 1], ACT.Copy).then_inc(w_ids_ready, 1)
                run(act, (list_rows, 0), (exps, 2), (elu_parts, 3), (first_ids, 0))

                def heavy_pair(i):
                    for q in range(2):
                        wait_alone(act, w_shifted, i * 2 + q + 1)
                        nc.scalar.activation(w_pr[q], w_sc[q], ACT.Exp).then_inc(w_exp_done, 1)
                        wait_alone(act, w_mixed, i * 2 + q + 1)
                        nc.scalar.activation(w_low[q], w_mix[q], ACT.Exp).then_inc(w_mixed_exp, 1)
                        wait_alone(act, w_mixed_exp, i * 2 + q + 1)
                        nc.scalar.activation(w_low[q], w_low[q], ACT.Relu, bias=1.0, scale=-1.0).then_inc(w_low_ready, 1)
                    wait_alone(act, w_ids_free, i + 1)
                    for q in range(2):
                        nc.scalar.activation(heavy_id[q][:], idf[:, bass.ds(i * 2 + 2 + q, 1)], ACT.Copy
                                             ).then_inc(w_ids_ready, 1)
                each_heavy_pair(act, heavy_pair)

            @block.vector
            def _(dve):
                def pack(ins, n):
                    ins.then_inc(pack_step, 1)
                    dve.wait_ge(pack_step, n)

                def per_tile(ap, n):
                    return ap.rearrange("p (t o) -> p t o", o=1).broadcast_to([P, TILES, n])

                def numbers(n):
                    return mcol[:, 0:n].rearrange("p (o m) -> p o m", o=1).broadcast_to([P, TILES, n])
                pack(nc.vector.tensor_scalar(heavy, keys_all[:, :, LIGHT], EMPTY, None, ALU.is_ge), 1)
                nc.vector.tensor_scalar(light[:], heavy, 0.5, None, ALU.is_lt)
                nc.vector.tensor_scalar(minus_ident[:], ident[:], -1.0, None, ALU.mult)
                nc.vector.memset(penalty[:, :, 0], 0.0)
                nc.vector.tensor_scalar(gone, keys_all[:, :, 0:LIGHT], EMPTY, -FAR, ALU.is_lt, ALU.mult)
                nc.vector.tensor_tensor(penalty[:, :, 1:PACKED], keys_all[:, :, 0:LIGHT], per_tile(rown[:], LIGHT),
                                        ALU.is_equal).then_inc(table_step, 1)
                nc.vector.tensor_scalar(row_number, rown[:], -1.0, KEY0 + 1.0, ALU.mult, ALU.add)
                nc.vector.tensor_reduce(most_due[:], due[:], AX.X, ALU.max)
                dve.wait_ge(table_step, 1)
                nc.vector.scalar_tensor_tensor(penalty[:, :, 1:PACKED], penalty[:, :, 1:PACKED], -FAR, gone,
                                               ALU.mult, ALU.add).then_inc(table_step, 1)
                dve.wait_ge(ranked, 2)
                pack(nc.vector.scalar_tensor_tensor(place, light[:], 2.0 * N, p_gT[:, 0:TILES], ALU.mult, ALU.add), 2)
                nc.vector.tensor_reduce(pairs[:, 0:1], p_cnt[:, 0:TILES], AX.X, ALU.add)
                pack(nc.vector.tensor_scalar(block_no, place, 0.5 - P / 2, 1.0 / P, ALU.add, ALU.mult), 3)
                pack(nc.vector.tensor_scalar(block_no, block_no, ROUND, None, ALU.add), 4)
                pack(nc.vector.tensor_scalar(block_no, block_no, -ROUND, None, ALU.add), 5)
                pack(nc.vector.scalar_tensor_tensor(place_in, block_no, -float(P), place, ALU.mult, ALU.add), 6)
                pack(nc.vector.tensor_scalar(pairs[:, 0:1], pairs[:, 0:1], P - 0.5, 0.5 / P, ALU.add, ALU.mult), 7)
                pack(nc.vector.tensor_scalar(pairs[:, 0:1], pairs[:, 0:1], ROUND, None, ALU.add), 8)
                pack(nc.vector.tensor_scalar(pairs[:, 0:1], pairs[:, 0:1], -ROUND, None, ALU.add), 9)
                nc.vector.tensor_copy(heavy_pairs[:], pairs[0:1, 0:1]).then_inc(pack_ready, 1)
                pack(nc.vector.tensor_tensor(hot_block, numbers(TILES), per_tile(block_no, TILES), ALU.is_equal), 10)
                nc.vector.tensor_tensor(hot_block, hot_block, per_tile(row_number, TILES), ALU.mult)
                nc.vector.tensor_tensor(hot_place, numbers(P), per_tile(place_in, P), ALU.is_equal).then_inc(spread, 1)

                def score(k, r):
                    dve.wait_ge(self_in[r], (k + 1) * 16)
                    dve.wait_ge(rows_in[r], (k + 1) * 16 * LIGHT)
                    nc.vector.tensor_tensor(sc[r][:], G[r][:, :, SR:SR + HEADS], heads(G[r][:, 0, SL:SL + HEADS], PACKED),
                                            ALU.add).then_inc(score_step, 1)

                def mask(k, r):
                    dve.wait_ge(score_step, num(k, r) * SCORE + 1)
                    out_of_it = penalty[:, bass.ds(num(k, r), 1), :].rearrange("p a (j o) -> p (a j) o", o=1
                                                                              ).broadcast_to([P, PACKED, HEADS])
                    nc.vector.tensor_tensor(sc[r][:], sc[r][:], out_of_it, ALU.add).then_inc(score_step, 1)

                def leaky(k, r):
                    dve.wait_ge(score_step, num(k, r) * SCORE + 2)
                    nc.vector.scalar_tensor_tensor(sc2[r][:], sc[r][:], SLOPE, sc[r][:], ALU.mult, ALU.max
                                                   ).then_inc(score_step, 1)

                def highest(k, r):
                    dve.wait_ge(score_step, num(k, r) * SCORE + 3)
                    nc.vector.tensor_reduce(mx[r][:], slots_first(sc2[r][:]), AX.X, ALU.max).then_inc(score_step, 1)

                def shift(k, r):
                    dve.wait_ge(score_step, num(k, r) * SCORE + 4)
                    nc.vector.tensor_tensor(sc[r][:], sc2[r][:], heads(mx[r][:], PACKED), ALU.subtract).then_inc(shifted, 1)

                def sum_exps(k, r):
                    dve.wait_ge(exp_done, num(k, r) + 1)
                    nc.vector.tensor_reduce(den[r][:], slots_first(pr[r][:]), AX.X, ALU.add).then_inc(mix_step, 1)

                def invert(k, r):
                    dve.wait_ge(mix_step, num(k, r) * MIX + 1)
                    nc.vector.reciprocal(rden[r][:], den[r][:]).then_inc(mix_step, 1)

                def weights(k, r):
                    dve.wait_ge(mix_step, num(k, r) * MIX + 2)
                    nc.vector.tensor_tensor(pr[r][:], pr[r][:], heads(rden[r][:], PACKED), ALU.mult).then_inc(mix_step, 1)

                def weighted(rows_ap, probs, n):
                    by_head = rows_ap[:, 0:n, 0:D].rearrange("p j (h k) -> p j h k", h=HEADS)
                    w = probs[:, 0:n, :].rearrange("p j (h o) -> p j h o", o=1).broadcast_to([P, n, HEADS, DK])
                    return nc.vector.tensor_tensor(by_head, by_head, w, ALU.mult)

                def total(dst, rows_ap, n):
                    return nc.vector.tensor_reduce(dst, rows_ap[:, 0:n, 0:D].rearrange("p j d -> p d j"), AX.X, ALU.add)

                def weigh(k, r):
                    dve.wait_ge(mix_step, num(k, r) * MIX + 3)
                    weighted(G[r], pr[r][:], PACKED).then_inc(mix_step, 1)

                def mix(k, r):
                    dve.wait_ge(mix_step, num(k, r) * MIX + 4)
                    total(mixv[r][:], G[r], PACKED).then_inc(mixed, 1)

                def add_x(k, r):
                    t = num(k, r)
                    if later_round(k):
                        wait_alone(dve, res_out[r], k * 16)
                    wait_alone(dve, elu_ready, t + 1)
                    nc.vector.tensor_tensor(res[r][:], p_elu[r][:, 0:D], x_tile(k, r), ALU.add).then_inc(res_ready, 1)

                def name_packed(k, r):
                    if not isinstance(k, int) or num(k, r) != NAMED:
                        return
                    dve.wait_ge(packed, 1)
                    nc.vector.memset(idf[:, TILES:TILES + 2], float(N))
                    pack(nc.vector.tensor_scalar(idf[:, 0:TILES], p_row[:, 0:TILES], 0.5, float(N + 1), ALU.is_lt, ALU.mult), 11)
                    pack(nc.vector.scalar_tensor_tensor(idf[:, 0:TILES], idf[:, 0:TILES], -1.0, p_row[:, 0:TILES], ALU.add, ALU.add), 12)
                    nc.vector.tensor_scalar(id_key, idf[:, 0:TILES], -1.0, KEY0, ALU.mult, ALU.add)
                    for q in range(2):
                        nc.vector.memset(w_x[q], 0.0)
                        nc.vector.memset(w_keys[q], 0.0)
                        nc.vector.memset(w_penalty[q], 0.0)
                        last = nc.vector.memset(HG[q][:, 0, :], 0.0)
                    last.then_inc(pack_ready, 1)
                dve.wait_ge(table_step, 2)
                run(dve, (score, 0), (sum_exps, 1), (mask, 0), (invert, 1), (leaky, 0), (weights, 1), (highest, 0),
                    (weigh, 1), (shift, 0), (add_x, 3), (mix, 1), (name_packed, 0))

                due_total = dve.alloc_register("heavy_due_total")
                dve.reg_mov(due_total, 0)

                def heavy_pair(i):
                    most = dve.value_load(most_due[0:1, 0:1], min_val=16 * ALWAYS, max_val=16 * SLOTS)
                    dve.reg_add(due_total, due_total, most)
                    dve.reg_add(due_total, due_total, 16)
                    for q in range(2):
                        heavy_tile(i, q, most)

                def heavy_tile(i, q, most):
                    def step(ins, n):
                        ins.then_inc(w_step, 1)
                        wait_alone(dve, w_step, (i * 2 + q) * HEAVY_STEPS + n)
                    wait_alone(dve, w_keys_in[q], (i + 1) * 16)
                    nc.vector.tensor_scalar(w_gone[q], w_keys[q], EMPTY, -FAR, ALU.is_lt, ALU.mult)
                    step(nc.vector.tensor_scalar(w_penalty[q][:, 1:CAND], w_keys[q], id_key[:, bass.ds(i * 2 + q, 1)], -FAR,
                                                 ALU.is_equal, ALU.mult), 1)
                    step(nc.vector.tensor_tensor(w_penalty[q][:, 1:CAND], w_penalty[q][:, 1:CAND], w_gone[q], ALU.add), 2)
                    wait_alone(dve, w_rows_in[q], dve.snap(due_total))
                    step(nc.vector.tensor_tensor(w_sc[q], HG[q][:, :, SR:SR + HEADS], heads(HG[q][:, 0, SL:SL + HEADS], CAND),
                                                 ALU.add), 3)
                    step(nc.vector.tensor_tensor(w_sc[q], w_sc[q], w_penalty[q].rearrange("p (j o) -> p j o", o=1)
                                                 .broadcast_to([P, CAND, HEADS]), ALU.add), 4)
                    step(nc.vector.scalar_tensor_tensor(w_sc2[q], w_sc[q], SLOPE, w_sc[q], ALU.mult, ALU.max), 5)
                    step(nc.vector.tensor_reduce(w_mx[q], slots_first(w_sc2[q]), AX.X, ALU.max), 6)
                    nc.vector.tensor_tensor(w_sc[q], w_sc2[q], heads(w_mx[q], CAND), ALU.subtract).then_inc(w_shifted, 1)
                    wait_alone(dve, w_exp_done, i * 2 + q + 1)
                    step(nc.vector.tensor_reduce(w_den[q], slots_first(w_pr[q]), AX.X, ALU.add), 7)
                    step(nc.vector.reciprocal(w_rden[q], w_den[q]), 8)
                    step(nc.vector.tensor_tensor(w_pr[q], w_pr[q], heads(w_rden[q], CAND), ALU.mult), 9)

                    def sum_rows(n):
                        step(weighted(HG[q], w_pr[q], n), 10)
                        total(w_mix[q], HG[q], n).then_inc(w_mixed, 1)
                    with dve.If(most > 16 * (ALWAYS + 3)):
                        with dve.If(most > 16 * (ALWAYS + 6)):
                            sum_rows(CAND)
                        with dve.Else():
                            sum_rows(ALWAYS + 7)
                    with dve.Else():
                        sum_rows(ALWAYS + 4)
                    wait_alone(dve, w_low_ready, i * 2 + q + 1)
                    step(nc.vector.scalar_tensor_tensor(w_res[q], w_mix[q], 0.0, w_low[q], ALU.max, ALU.subtract), 11)
                    wait_alone(dve, w_x_in[q], (i + 1) * 16)
                    nc.vector.tensor_tensor(w_res[q], w_res[q], w_x[q], ALU.add).then_inc(w_res_ready, 1)
                each_heavy_pair(dve, heavy_pair)

        e_free, e_in, e_block_in, e_block_free = sem("e_free"), sem("e_in"), sem("e_block_in"), sem("e_block_free")
        e_diag, e_spread, e_args, e_exps, e_turned, e_copied, e_product = (
            sem(f"e_{n}") for n in ("diag", "spread", "args", "exps", "turned", "copied", "product"))
        e_step, e_tile_step, e_low, e_low_exp, e_res, e_out = (
            sem(f"e_{n}") for n in ("step", "tile_step", "low", "low_exp", "res", "out"))
        BLOCKS = HALF // P
        E_STEPS, E_TILE_STEPS = 12, 7
        off = [2 * (HALF + SENT)]

        def take(width):
            off[0] += width
            return bigf[:, off[0] - width:off[0]]
        e_self, e_rows, e_mask, e_neg = take(ROW), take(ROW), take(P), take(P)
        e_dg, e_raw, e_sc, e_p, e_pT = (take(HEADS * P) for _ in range(5))
        e_rel, e_mx, e_bm, e_new, e_dc, e_corr, e_sum, e_l = (take(HEADS) for _ in range(8))
        e_acc, e_lowv = take(D), take(D)

        def per_head(ap):
            return ap.rearrange("p (h m) -> p h m", h=HEADS)

        def over_columns(ap, n):
            return ap.rearrange("p (h o) -> p h o", o=1).broadcast_to([P, HEADS, n])

        def every_head(ap):
            return ap.rearrange("p (o m) -> p o m", o=1).broadcast_to([P, HEADS, P])

        def each_block(eng, i, body):
            for s in range(2):
                with eng.Fori(0, BLOCKS) as b:
                    body((i * 2 + s) * BLOCKS + b, s, b)

        with nc.Block() as block:

            @block.sync
            def _(sp):
                def load(i, t):
                    sp.wait_ge(e_free, i + 1)
                    for s in range(2):
                        sp.dma_start(A[s][:, 0:HALF], adj[bass.ds(t * P, P), s * HALF:(s + 1) * HALF]).then_inc(e_in, 16)
                    sp.dma_start(e_self, row_dram[bass.ds(t * P, P), :]).then_inc(e_in, 16)

                    def block_rows(n, s, b):
                        sp.wait_ge(e_block_free, n + 1)
                        sp.dma_start(e_rows, row_dram[bass.ds(b * P + s * HALF, P), :]).then_inc(e_block_in, 16)
                    each_block(sp, i, block_rows)
                    sp.wait_ge(e_res, i + 1)
                    sp.dma_start(out[bass.ds(t * P, P), :], res[0][:]).then_inc(e_out, 16)
                    sp.wait_ge(e_out, (i + 1) * 16)
                    sp.sem_inc(e_free, 1)
                each_dense_tile(sp, load)

            @block.vector
            def _(dve):
                dve.sem_inc(e_free, 1)
                dve.sem_inc(e_block_free, 1)

                def attend(i, t):
                    def tile_step(ins, n):
                        ins.then_inc(e_tile_step, 1)
                        wait_alone(dve, e_tile_step, i * E_TILE_STEPS + n)
                    dve.wait_ge(e_in, (i + 1) * 16 * 3)
                    nc.vector.memset(e_l, 1.0)
                    nc.vector.tensor_copy(e_acc, e_self[:, 0:D])
                    nc.vector.tensor_scalar(e_rel[:, 0:1], rown[:, bass.ds(t, 1)], -1.0, KEY0, ALU.mult, ALU.add)
                    tile_step(nc.vector.tensor_tensor(e_bm, e_self[:, SR:SR + HEADS], e_self[:, SL:SL + HEADS], ALU.add), 1)
                    tile_step(nc.vector.scalar_tensor_tensor(e_mx, e_bm, SLOPE, e_bm, ALU.mult, ALU.max), 2)

                    def one_block(n, s, b):
                        def step(ins, m):
                            ins.then_inc(e_step, 1)
                            wait_alone(dve, e_step, n * E_STEPS + m)
                        wait_alone(dve, e_block_in, (n + 1) * 16)
                        nc.vector.tensor_tensor(per_head(e_dg), every_head(ident[:]), over_columns(e_rows[:, SR:SR + HEADS], P),
                                                ALU.mult).then_inc(e_diag, 1)
                        step(nc.vector.scalar_tensor_tensor(e_mask, mcol[:], e_rel[:, 0:1], A[s][:, bass.ds(b * P, P)],
                                                            ALU.not_equal, ALU.mult), 1)
                        nc.vector.tensor_scalar(e_rel[:, 0:1], e_rel[:, 0:1], -float(P), None, ALU.add)
                        step(nc.vector.tensor_scalar(e_neg, e_mask, -1.0, FAR, ALU.add, ALU.mult), 2)
                        wait_alone(dve, e_spread, n + 1)
                        step(nc.vector.tensor_tensor(per_head(e_raw), per_head(p_u[0][:]), over_columns(e_self[:, SL:SL + HEADS], P),
                                                     ALU.add), 3)
                        step(nc.vector.scalar_tensor_tensor(e_sc, e_raw, SLOPE, e_raw, ALU.mult, ALU.max), 4)
                        step(nc.vector.tensor_tensor(per_head(e_raw), per_head(e_sc), every_head(e_neg), ALU.add), 5)
                        step(nc.vector.tensor_reduce(e_bm, per_head(e_raw), AX.X, ALU.max), 6)
                        step(nc.vector.tensor_tensor(e_new, e_mx, e_bm, ALU.max), 7)
                        nc.vector.tensor_tensor(e_dc, e_mx, e_new, ALU.subtract)
                        step(nc.vector.tensor_tensor(per_head(e_sc), per_head(e_raw), over_columns(e_new, P), ALU.subtract), 8)
                        nc.vector.tensor_copy(e_mx, e_new).then_inc(e_args, 1)
                        wait_alone(dve, e_exps, n + 1)
                        nc.vector.tensor_tensor(per_head(e_acc), per_head(e_acc), over_columns(e_corr, DK), ALU.mult)
                        step(nc.vector.tensor_tensor(e_l, e_l, e_corr, ALU.mult), 9)
                        step(nc.vector.tensor_reduce(e_sum, per_head(e_p), AX.X, ALU.add), 10)
                        step(nc.vector.tensor_tensor(e_l, e_l, e_sum, ALU.add), 11)
                        wait_alone(dve, e_product, n + 1)
                        nc.vector.tensor_tensor(e_acc, e_acc, p_u[2][:, 0:D], ALU.add).then_inc(e_block_free, 1)
                        wait_alone(dve, e_block_free, n + 2)
                        dve.sem_inc(e_step, 1)
                    each_block(dve, i, one_block)
                    tile_step(nc.vector.reciprocal(e_sum, e_l), 3)
                    tile_step(nc.vector.tensor_tensor(per_head(e_acc), per_head(e_acc), over_columns(e_sum, DK), ALU.mult), 4)
                    nc.vector.tensor_scalar(e_lowv, e_acc, 0.0, None, ALU.min).then_inc(e_low, 1)
                    tile_step(nc.vector.scalar_tensor_tensor(res[0][:], e_acc, 0.0, x_at(t), ALU.max, ALU.add), 5)
                    wait_alone(dve, e_low_exp, i + 1)
                    tile_step(nc.vector.scalar_tensor_tensor(res[0][:], e_lowv, -1.0, res[0][:], ALU.add, ALU.add), 6)
                    dve.sem_inc(e_tile_step, 1)
                    dve.sem_inc(e_res, 1)
                each_dense_tile(dve, attend)

            @block.scalar
            def _(act):
                def exps(i, t):
                    def one_block(n, s, b):
                        act.wait_ge(e_args, n + 1)
                        nc.scalar.activation(e_corr, e_dc, ACT.Exp)
                        nc.scalar.activation(e_p, e_sc, ACT.Exp).then_inc(e_exps, 1)
                        act.wait_ge(e_turned, n + 1)
                        nc.scalar.copy(e_pT, p_u[1][:]).then_inc(e_copied, 1)
                    each_block(act, i, one_block)
                    act.wait_ge(e_low, i + 1)
                    nc.scalar.activation(e_lowv, e_lowv, ACT.Exp).then_inc(e_low_exp, 1)
                each_dense_tile(act, exps)

            @block.tensor
            def _(pe):
                def products(i, t):
                    def one_block(n, s, b):
                        pe.wait_ge(e_diag, n + 1)
                        nc.tensor.matmul(p_u[0][:], ones[:], e_dg, start=True, stop=True).then_inc(e_spread, 1)
                        pe.wait_ge(e_exps, n + 1)
                        for q in range(HEADS):
                            last = nc.tensor.transpose(p_u[1][:, q * P:(q + 1) * P], e_p[:, q * P:(q + 1) * P], ident[:])
                        last.then_inc(e_turned, 1)
                        pe.wait_ge(e_copied, n + 1)
                        for q in range(HEADS):
                            last = nc.tensor.matmul(p_u[2][:, q * DK:(q + 1) * DK], e_pT[:, q * P:(q + 1) * P],
                                                    e_rows[:, q * DK:(q + 1) * DK], start=True, stop=True)
                        last.then_inc(e_product, 1)
                    each_block(pe, i, one_block)
                each_dense_tile(pe, products)


_INS = ["x", "adj", "L0_gnn_w_self", "L0_gnn_w_neigh", "L1_gnn_W", "L1_gnn_a_l", "L1_gnn_a_r"]


def kernel(**inputs):
    import numpy as _np
    import concourse.bacc as _bacc
    from concourse import mybir as _mybir
    from concourse.bass_utils import run_bass_kernel_spmd as _run

    nc = _bacc.Bacc("TRN2", target_bir_lowering=False, num_devices=1)
    arrays, args = {}, []
    for name in _INS:
        a = _np.ascontiguousarray(inputs[name])
        arrays[f"in_{name}_dram"] = a
        args.append(nc.dram_tensor(f"in_{name}_dram", a.shape, _mybir.dt.from_np(a.dtype), kind="ExternalInput").ap())
    args.append(nc.dram_tensor("out_0_dram", inputs["x"].shape, _mybir.dt.float32, kind="ExternalOutput").ap())
    preln_gnn_gat_kernel(nc, *args)
    r = _run(nc, [arrays], core_ids=[0])
    return r.results[0]["out_0_dram"]
```
